# Optimizing a Trainium2 kernel written in Bass

```python
import numpy as np
import jax
import jax.numpy as jnp

def _softmax(x, axis=-1):
    return jax.nn.softmax(x, axis=axis)

def _gelu(x):
    return jax.nn.gelu(x, approximate=True)

def _silu(x):
    return jax.nn.silu(x)

def _sigmoid(x):
    return jax.nn.sigmoid(x)

def _layernorm(x, axis=-1, eps=1e-05):
    m = jnp.mean(x, axis=axis, keepdims=True)
    v = jnp.var(x, axis=axis, keepdims=True)
    return (x - m) / jnp.sqrt(v + eps)

def _scatter_add(tgt, idx, src, axis=0):
    return tgt.at[idx].add(src)

def _segment_sum(src, seg, n):
    return jax.ops.segment_sum(src, seg, n)
kernel_name = 'mk_macaron_d1_jaxref_r8_fa618f'

def setup_inputs(seed: int=0):
    np.random.seed(seed)
    _w = jnp.asarray

    def _L0_attn_setup():
        import jax, jax.numpy as jnp
        import numpy as np
        EMBED_DIM = 128
        NUM_HEADS = 16
        HEAD_DIM = EMBED_DIM // NUM_HEADS
        KERNEL_SIZE = 64
        B, L = (2, 256)
        key = jax.random.key(seed)
        ks = jax.random.split(key, 6)
        x = jax.random.normal(ks[0], (B, L, EMBED_DIM), dtype=jnp.float32)
        qkv_w = jax.random.normal(ks[1], (EMBED_DIM, 3 * EMBED_DIM), dtype=jnp.float32) / np.sqrt(EMBED_DIM)
        qkv_b = jnp.zeros((3 * EMBED_DIM,), dtype=jnp.float32)
        out_w = jax.random.normal(ks[2], (EMBED_DIM, EMBED_DIM), dtype=jnp.float32) / np.sqrt(EMBED_DIM)
        out_b = jnp.zeros((EMBED_DIM,), dtype=jnp.float32)
        proj = jax.random.normal(ks[3], (NUM_HEADS, HEAD_DIM, KERNEL_SIZE), dtype=jnp.float32) / np.sqrt(HEAD_DIM)
        return {'x': x, 'qkv_w': qkv_w, 'qkv_b': qkv_b, 'out_w': out_w, 'out_b': out_b, 'proj': proj}
    _L0_attn_in = _L0_attn_setup()

    def _L0_ffn_setup():
        import jax, jax.numpy as jnp
        import numpy as np
        B, S, D, F, E = (8, 128, 128, 512, 8)
        EPS = 1e-05
        key = jax.random.key(seed)
        ks = jax.random.split(key, 4)
        s = 0.02
        return {'input_features': jax.random.normal(ks[0], (B, S, D), jnp.float32), 'centroids': jax.random.normal(ks[1], (E, D), jnp.float32) * 0.1, 'ln_g': jnp.ones((E, D), jnp.float32), 'ln_b': jnp.zeros((E, D), jnp.float32), 'w1': jax.random.normal(ks[2], (E, D, F), jnp.float32) * s, 'b1': jnp.zeros((E, F), jnp.float32), 'w2': jax.random.normal(ks[3], (E, F, D), jnp.float32) * s, 'b2': jnp.zeros((E, D), jnp.float32)}
    _L0_ffn_in = _L0_ffn_setup()
    _d = {'L0_attn_x': _L0_attn_in['x'], 'L0_attn_qkv_w': _L0_attn_in['qkv_w'], 'L0_attn_qkv_b': _L0_attn_in['qkv_b'], 'L0_attn_out_w': _L0_attn_in['out_w'], 'L0_attn_out_b': _L0_attn_in['out_b'], 'L0_attn_proj': _L0_attn_in['proj'], 'L0_ffn_centroids': _L0_ffn_in['centroids'], 'L0_ffn_ln_g': _L0_ffn_in['ln_g'], 'L0_ffn_ln_b': _L0_ffn_in['ln_b'], 'L0_ffn_w1': _L0_ffn_in['w1'], 'L0_ffn_b1': _L0_ffn_in['b1'], 'L0_ffn_w2': _L0_ffn_in['w2'], 'L0_ffn_b2': _L0_ffn_in['b2']}
    _x0 = _d['L0_attn_x']
    _d['L0_attn_x'] = jax.random.normal(jax.random.fold_in(jax.random.key(seed), 1), (2, 1024, 128), dtype=_x0.dtype)
    del _x0
    return _d

def reference(L0_attn_x, L0_attn_qkv_w, L0_attn_qkv_b, L0_attn_out_w, L0_attn_out_b, L0_attn_proj, L0_ffn_centroids, L0_ffn_ln_g, L0_ffn_ln_b, L0_ffn_w1, L0_ffn_b1, L0_ffn_w2, L0_ffn_b2):

    def _L0_attn_ref(x, qkv_w, qkv_b, out_w, out_b, proj):
        import jax, jax.numpy as jnp
        import numpy as np
        EMBED_DIM = 128
        NUM_HEADS = 16
        HEAD_DIM = EMBED_DIM // NUM_HEADS
        KERNEL_SIZE = 64
        B, L = (2, 256)
        Bn, Ln, E = x.shape
        H, D, M = proj.shape
        qkv = x @ qkv_w + qkv_b
        q, k, v = jnp.split(qkv, 3, axis=-1)
        q = q.reshape(Bn, Ln, H, D).transpose(0, 2, 1, 3)
        k = k.reshape(Bn, Ln, H, D).transpose(0, 2, 1, 3)
        v = v.reshape(Bn, Ln, H, D).transpose(0, 2, 1, 3)
        q_prime = jax.nn.relu(jnp.einsum('bhld,hdm->bhlm', q, proj))
        k_prime = jax.nn.relu(jnp.einsum('bhld,hdm->bhlm', k, proj))
        kv_prod = jnp.einsum('bhlm,bhld->bhlmd', k_prime, v)
        kv_cumsum = jnp.cumsum(kv_prod, axis=2)
        context = jnp.einsum('bhlm,bhlmd->bhld', q_prime, kv_cumsum)
        k_cumsum = jnp.cumsum(k_prime, axis=2)
        norm = jnp.einsum('bhlm,bhlm->bhl', q_prime, k_cumsum)
        out = context / (norm[..., None] + 1e-06)
        out = out.transpose(0, 2, 1, 3).reshape(Bn, Ln, E)
        return out @ out_w + out_b

    def _L0_ffn_ref(input_features, centroids, ln_g, ln_b, w1, b1, w2, b2):
        import jax, jax.numpy as jnp
        import numpy as np
        B, S, D, F, E = (8, 128, 128, 512, 8)
        EPS = 1e-05
        x = input_features.reshape(-1, D)
        aff = jax.lax.stop_gradient(x @ centroids.T)
        eid = jnp.argmax(aff, axis=-1)
        alpha = jax.nn.sigmoid(jnp.sum(x * centroids[eid], axis=-1, keepdims=True))
        mu = jnp.mean(x, axis=-1, keepdims=True)
        var = jnp.mean((x - mu) ** 2, axis=-1, keepdims=True)
        xn = (x - mu) * jax.lax.rsqrt(var + EPS)
        xln = xn * ln_g[eid] + ln_b[eid]
        onehot = jax.nn.one_hot(eid, E, dtype=x.dtype)
        ffn = jnp.zeros_like(x)
        for e in range(E):
            h = jax.nn.relu(xln @ w1[e] + b1[e])
            ffn = ffn + onehot[:, e:e + 1] * (h @ w2[e] + b2[e])
        out = x + alpha * ffn
        return out.reshape(input_features.shape)
    x = L0_attn_x
    x = x + 0.5 * _L0_ffn_ref(_layernorm(x, axis=-1), L0_ffn_centroids, L0_ffn_ln_g, L0_ffn_ln_b, L0_ffn_w1, L0_ffn_b1, L0_ffn_w2, L0_ffn_b2)
    x = x + _L0_attn_ref(_layernorm(x, axis=-1), L0_attn_qkv_w, L0_attn_qkv_b, L0_attn_out_w, L0_attn_out_b, L0_attn_proj)
    x = x + 0.5 * _L0_ffn_ref(_layernorm(x, axis=-1), L0_ffn_centroids, L0_ffn_ln_g, L0_ffn_ln_b, L0_ffn_w1, L0_ffn_b1, L0_ffn_w2, L0_ffn_b2)
    return x

_drawn_inputs = setup_inputs


def setup_inputs(seed=0):
    import zlib

    import numpy as np

    out = dict(_drawn_inputs(seed))
    spreads = {'L0_attn_qkv_b': (0.0, 0.1),
     'L0_attn_out_b': (0.0, 0.1),
     'L0_ffn_ln_g': (1.0, 0.6),
     'L0_ffn_ln_b': (0.0, 2.0),
     'L0_ffn_b1': (0.0, 0.558),
     'L0_ffn_b2': (0.0, 0.1)}
    factors = {}
    for name, (base, spread) in spreads.items():
        noise = np.random.default_rng([zlib.crc32(name.encode()), seed]).standard_normal(out[name].shape)
        drawn = base * np.exp(spread * noise) if base else spread * noise
        out[name] = jnp.asarray(drawn.astype(out[name].dtype))
    for name, factor in factors.items():
        out[name] = (out[name] * factor).astype(out[name].dtype)
    return out
```

```python
from contextlib import ExitStack

import concourse.bass as bass
from concourse import mybir

P = 128
F32 = mybir.dt.float32
I32 = mybir.dt.int32
ALU = mybir.AluOpType
ACT = mybir.ActivationFunctionType
AX_X = mybir.AxisListType.X
LN_EPS = 1e-5
DEN_EPS = 1e-6


class FfnSignals:

    def __init__(self, sem, n):
        self.stats1 = sem(f"stats1_{n}")
        self.aggr1 = sem(f"aggr1_{n}")
        self.dev1 = sem(f"dev1_{n}")
        self.rstd1 = sem(f"rstd1_{n}")
        self.norm1 = sem(f"norm1_{n}")
        self.stats2 = sem(f"stats2_{n}")
        self.aggr2 = sem(f"aggr2_{n}")
        self.dev2 = sem(f"dev2_{n}")
        self.rstd2 = sem(f"rstd2_{n}")
        self.norm2 = sem(f"norm2_{n}")
        self.f_turned = sem(f"f_turned_{n}")
        self.f_turned_sb = sem(f"f_turned_sb_{n}")
        self.affinity = sem(f"affinity_{n}")
        self.gate = sem(f"gate_{n}")
        self.route = sem(f"route_{n}")
        self.onehot = sem(f"onehot_{n}")
        self.counts = sem(f"counts_{n}")
        self.table = sem(f"table_{n}")
        self.positions = sem(f"positions_{n}")
        self.scattered = sem(f"scattered_{n}")
        self.weights = sem(f"weights_{n}")
        self.vectors = sem(f"vectors_{n}")
        self.rows_turned = sem(f"rows_turned_{n}")
        self.inputs = sem(f"inputs_{n}")
        self.up = sem(f"up_{n}")
        self.relu_act = sem(f"relu_act_{n}")
        self.relu_dve = sem(f"relu_dve_{n}")
        self.down = sem(f"down_{n}")
        self.rows_out = sem(f"rows_out_{n}")
        self.mixed = sem(f"mixed_{n}")
        self.result = sem(f"result_{n}")
        self.rows_loaded = [sem(f"rows_loaded{r}_{n}") for r in range(4)]
        self.rows_stored = [sem(f"rows_stored{r}_{n}") for r in range(4)]


def macaron_block(nc, x_in, qkv_w, qkv_b, out_w, out_b, proj, centroids, ln_g, ln_b, w1, b1, w2, b2, out):
    B, L, D = x_in.shape
    H, HD, M = proj.shape
    E, _, F = w1.shape
    NT = B * L // P
    FC = F // P
    NS = (B * L + E * (P - 1)) // P
    SPARE = 2
    NB = 4
    PAIRS = H // 2
    CHUNKS = L // P
    GROUPS = CHUNKS // NB
    assert D == P and F == 4 * P and H * HD == P and 2 * M == P and B * L % P == 0 and GROUPS == 2 and PAIRS == 8
    assert NS % 4 == 3
    ZERO_DMAS = (NS + SPARE) // 5
    assert ZERO_DMAS * 5 == NS + SPARE

    AGGR = 6

    W1, W2, B2, B1, GG, BB = 0, F, F + FC * P, F + FC * P + D, F + FC * P + D + FC, F + FC * P + D + FC + 1
    REC = BB + 1
    R_B1, R_G, R_B, R_C, R_QB, NR = 0, E * FC, E * FC + E, E * FC + 2 * E, E * FC + 3 * E, E * FC + 3 * E + 2

    sorted_in = nc.dram_tensor("sorted_in", [(NS + SPARE) * P, D], F32, kind="Internal").ap()
    sorted_out = nc.dram_tensor("sorted_out", [NS * P, D], F32, kind="Internal").ap()

    ctx = ExitStack()
    with ctx:
        def sb(name, shape, dt=F32):
            return ctx.enter_context(nc.sbuf_tensor(name, shape, dt))

        def sem(name):
            return ctx.enter_context(nc.semaphore(name))

        psum = ctx.enter_context(nc.psum_tensor("psum", [P, 8, 512], F32))

        ident = sb("ident", [P, P])
        before = sb("before", [P, P])
        causal = sb("causal", [P, P])
        ones = sb("ones", [P, P])
        zero_rows = sb("zero_rows", [P, 5 * D])
        head_block = sb("head_block", [P, H])
        first_rank = sb("first_rank", [P, E])
        tile_edges = sb("tile_edges", [P, NT])
        slots = sb("slots", [P, NS + 1])
        eps_col = sb("eps_col", [P, 1])
        rows = sb("rows", [NR, P])
        cols = sb("cols", [P, NR])
        records = sb("records", [P, E, REC])
        qkv_sb = sb("qkv_sb", [P, 3 * D])
        v_bias = sb("v_bias", [P, D])
        outw_sb = sb("outw_sb", [P, D])
        out_bias = sb("out_bias", [P, D])
        proj_sb = sb("proj_sb", [P, M])
        proj_wide = sb("proj_wide", [P, H, M])
        w_turned = sb("w_turned", [P, 2, P])
        w_feat = sb("w_feat", [P, 2, H * M])
        b_feat = sb("b_feat", [P, PAIRS, 2])

        x = sb("x", [P, NT + NB, D])
        f = sb("f", [P, NT, D])
        xn = sb("xn", [P, NT, D])
        mix = xn
        stats = sb("stats", [P, NT, 6])
        mv1 = sb("mv1", [P, 2, NT])
        mv2 = sb("mv2", [P, 2, NT])
        halves = sb("halves", [P, 4, NB])
        dev = sb("dev", [P, NT])
        rstd = sb("rstd", [P, NT])
        stats_b = sb("stats_b", [P, NT, 6])
        dev_b = sb("dev_b", [P, NT])
        rstd_b = sb("rstd_b", [P, NT])
        best = sb("best", [P, NT])
        alpha = sb("alpha", [P, NT])
        is_best = sb("is_best", [P, NT, E])
        ranked = sb("ranked", [P, NT, E])
        best_rank = sb("best_rank", [P, NT])
        onehot = sb("onehot", [P, E, NT])
        n_e = sb("n_e", [P, E])
        over = sb("over", [P, E, NT])
        tiles_e = sb("tiles_e", [P, E])
        tiles_upto = sb("tiles_upto", [P, E])
        run_incl = sb("run_incl", [P, E * NT])
        run_excl = sb("run_excl", [P, E, NT])
        start_e = sb("start_e", [P, E])
        shift_e = sb("shift_e", [P, E])
        offset = sb("offset", [P, E, NT])
        rank_at = sb("rank_at", [P, E, NT])
        chosen_at = sb("chosen_at", [P, E, NT])
        pos_f = sb("pos_f", [P, NT])
        pos = sb("pos", [P, NT], I32)
        passed = sb("passed", [P, NS + 1, E])
        owner_f = sb("owner_f", [P, NS + 1])
        owner_at = sb("owner_at", [P, NS + 1])
        owner = sb("owner", [P, NS + 1], I32)

        rows_in = sb("rows_in", [P, 4, D])
        rec = sb("rec", [P, 4, REC])
        lnT = sb("lnT", [P, 2, P])
        hid = sb("hid", [P, 2, FC, P])
        rows_out = sb("rows_out", [P, 4, D])

        xa = sb("xa", [P, NB, D])
        xaT = sb("xaT", [P, NB, P])
        qT = sb("qT", [P, PAIRS, NB * P])
        kT = sb("kT", [P, PAIRS, NB * P])
        f_turned = qT[:, :, :].rearrange("p r t -> p (r t)")[:, 0:NT * P].rearrange("p (t q) -> p t q", q=P)
        v_raw = sb("v_raw", [P, NB, D])
        v_pair = sb("v_pair", [P, GROUPS, NB, PAIRS, 32])
        v_head = sb("v_head", [P, GROUPS, NB, PAIRS, 2, 32])
        k_rows = sb("k_rows", [P, PAIRS, P])
        scores = sb("scores", [P, 2, 4, NB, P])
        o_sb = sb("o_sb", [P, 2, P])
        den = sb("den", [P, PAIRS, 2])
        inv_den = sb("inv_den", [P, PAIRS, 2])
        heads_out = sb("heads_out", [P, PAIRS, 2, HD])
        heads_T = sb("heads_T", [P, P])
        proj_out = sb("proj_out", [P, D])
        stateT = sb("stateT", [P, 2, P])
        state = sb("state", [P, PAIRS, 32])

        x_loaded = [sem(f"x_loaded{q}") for q in range(NT // NB)]
        small_loaded = sem("small_loaded")
        attn_loaded = sem("attn_loaded")
        experts_loaded = sem("experts_loaded")
        zeros_ready = sem("zeros_ready")
        zeroed = sem("zeroed")
        filled = sem("filled")
        consts = sem("consts")
        cols_psum = sem("cols_psum")
        cols_ready = sem("cols_ready")
        records_ready = sem("records_ready")
        wide_ready = sem("wide_ready")
        w_turned_psum = sem("w_turned_psum")
        w_turned_sb = sem("w_turned_sb")
        w_feat_psum = sem("w_feat_psum")
        w_feat_sb = sem("w_feat_sb")
        b_feat_psum = sem("b_feat_psum")
        gathered = [sem(f"gathered{t}") for t in range(NT)]
        out_stored = sem("out_stored")
        ffn = [FfnSignals(sem, n) for n in range(2)]
        a_stats, a_aggr, a_dev, a_rstd, a_norm = (sem(f"a_{s}") for s in ("stats", "aggr", "dev", "rstd", "norm"))
        wide_done = sem("wide_done")
        wide_read = sem("wide_read")
        v_ready = sem("v_ready")
        scored = sem("scored")
        masked = sem("masked")
        o_done = sem("o_done")
        o_read = sem("o_read")
        o_turned = sem("o_turned")
        den_ready = sem("den_ready")
        inv_ready = sem("inv_ready")
        heads_ready = sem("heads_ready")
        heads_turned = sem("heads_turned")
        heads_T_ready = sem("heads_T_ready")
        projected = sem("projected")
        projected_sb = sem("projected_sb")
        residual = sem("residual")
        stateT_done = sem("stateT_done")
        stateT_added = sem("stateT_added")
        state_turned = sem("state_turned")
        state_ready = sem("state_ready")

        block = ctx.enter_context(nc.Block())

        def ring(o):
            return (1 + o) % 4

        def ring_value(i, o):
            return i * 4 + (12 + 16 * ((o + 1) // 4))

        def early(i, o, n):
            return isinstance(i, int) and i + o < n

        LOOP_FROM, LOOP_TO = 5, NS - 2

        WIDE_G = 2 + 2 * PAIRS + 2 * NB
        WIDE_B = GROUPS * WIDE_G - 2
        KEY_ROWS = 1 + 2 * PAIRS

        def wide(b, g, idx):
            return b * WIDE_B + (1 + WIDE_G * g + idx)

        def turn_idx(g):
            return WIDE_G - 1 if g < GROUPS - 1 else WIDE_G - 3

        @block.sync
        def _(sp):
            for q in range(NT // NB):
                sp.dma_start(x[:, q * NB:(q + 1) * NB, :],
                             x_in.rearrange("b (t p) d -> p (b t) d", p=P)[:, q * NB:(q + 1) * NB, :]
                             ).then_inc(x_loaded[q], 16)
            sp.wait_ge(zeros_ready, 1)
            for q in range(ZERO_DMAS):
                sp.dma_start(sorted_in.rearrange("(t p) d -> p t d", p=P)[:, 5 * q:5 * q + 5, :],
                             zero_rows[:, :].rearrange("p (t d) -> p t d", d=D)).then_inc(zeroed, 16)

            for n in range(2):
                s = ffn[n]

                def load(i, o):
                    if not early(i, o, 4):
                        sp.wait_ge(s.rows_turned, i + (o - 3))
                    sp.dma_start(rows_in[:, ring(o), :], sorted_in[bass.ds((i + o) * P, P), :]
                                 ).then_inc(s.rows_loaded[ring(o)], 16)

                def store(i, o):
                    sp.wait_ge(s.rows_out, i + (o + 1))
                    sp.dma_start(sorted_out[bass.ds((i + o) * P, P), :], rows_out[:, ring(o), :]
                                 ).then_inc(s.rows_stored[ring(o)], 16)

                sp.wait_ge(s.scattered, 16 * NT)
                for o in range(-1, 3):
                    load(1, o)
                for o in range(-1, 4):
                    load(1, o + 4)
                    store(1, o)
                with sp.Fori(LOOP_FROM, LOOP_TO - 3, 4) as i:
                    for o in range(4):
                        load(i, o + 4)
                        store(i, o)
                for o in range(2):
                    store(LOOP_TO, o)
                for o in (2, 3):
                    sp.wait_ge(s.rows_loaded[ring(o)], ring_value(LOOP_TO, o))
                if n == 1:
                    for q in range(NT // NB):
                        sp.wait_ge(s.result, NB * (q + 1))
                        sp.dma_start(out.rearrange("b (t p) d -> p (b t) d", p=P)[:, q * NB:(q + 1) * NB, :],
                                     x[:, q * NB:(q + 1) * NB, :]).then_inc(out_stored, 16)
                    sp.wait_ge(out_stored, 16 * (NT // NB))

        @block.gpsimd
        def _(pool):
            nc.gpsimd.memset(zero_rows[:, :], 0.0).then_inc(zeros_ready, 1)
            fills = [(ident, 0.0), (before, 1.0), (causal, 1.0), (ones, 1.0), (head_block, 1.0)]
            for n, (t, value) in enumerate(fills):
                nc.gpsimd.memset(t[:, :], value).then_inc(filled, 1)
            nc.gpsimd.memset(eps_col[:, :], LN_EPS).then_inc(filled, 1)
            pool.wait_ge(filled, 6)
            nc.gpsimd.affine_select(out=ident[:, :], in_=ident[:, :], compare_op=ALU.not_equal, fill=1.0, base=0,
                                    pattern=[[-1, P]], channel_multiplier=1).then_inc(consts, 1)
            nc.gpsimd.affine_select(out=before[:, :], in_=before[:, :], compare_op=ALU.is_gt, fill=0.0, base=0,
                                    pattern=[[1, P]], channel_multiplier=-1).then_inc(consts, 1)
            nc.gpsimd.affine_select(out=causal[:, :], in_=causal[:, :], compare_op=ALU.is_ge, fill=0.0, base=0,
                                    pattern=[[1, P]], channel_multiplier=-1).then_inc(consts, 1)
            nc.gpsimd.iota(first_rank[:, :], pattern=[[-1, E]], base=E, channel_multiplier=0,
                           allow_small_or_imprecise_dtypes=True).then_inc(consts, 1)
            nc.gpsimd.iota(tile_edges[:, :], pattern=[[P, NT]], base=0, channel_multiplier=0,
                           allow_small_or_imprecise_dtypes=True).then_inc(consts, 1)
            nc.gpsimd.iota(slots[:, :], pattern=[[1, NS + 1]], base=0, channel_multiplier=0,
                           allow_small_or_imprecise_dtypes=True).then_inc(consts, 1)
            nc.gpsimd.affine_select(out=head_block[:, :], in_=head_block[:, :], compare_op=ALU.is_ge, fill=0.0,
                                    base=0, pattern=[[-HD, H]], channel_multiplier=1).then_inc(consts, 1)
            pool.wait_ge(consts, 7)
            nc.gpsimd.affine_select(out=head_block[:, :], in_=head_block[:, :], compare_op=ALU.is_ge, fill=0.0,
                                    base=HD - 1, pattern=[[HD, H]], channel_multiplier=-1).then_inc(consts, 1)
            nc.gpsimd.memset(x[:, NT:NT + NB, :], 0.0).then_inc(filled, 1)
            nc.gpsimd.memset(v_pair[:, :, :, :, :], 0.0).then_inc(filled, 1)
            nc.gpsimd.memset(v_head[:, :, :, :, :, :], 0.0).then_inc(filled, 1)
            pool.wait_ge(filled, 9)
            for g in range(GROUPS):
                for a in range(2):
                    nc.gpsimd.memset(v_pair[:, g, :, :, 9 * a + HD:9 * a + HD + 1], 1.0).then_inc(filled, 1)
                    nc.gpsimd.memset(v_head[:, g, :, :, a, 9 * a + HD:9 * a + HD + 1], 1.0).then_inc(filled, 1)
            pool.wait_ge(cols_ready, 1)
            nc.gpsimd.tensor_copy(records[:, :, B1:B1 + FC],
                                  cols[:, R_B1:R_B1 + E * FC].rearrange("p (e c) -> p e c", c=FC)
                                  ).then_inc(records_ready, 1)
            nc.gpsimd.tensor_copy(records[:, :, GG:GG + 1],
                                  cols[:, R_G:R_G + E].rearrange("p (e c) -> p e c", c=1)).then_inc(records_ready, 1)
            nc.gpsimd.tensor_copy(records[:, :, BB:BB + 1],
                                  cols[:, R_B:R_B + E].rearrange("p (e c) -> p e c", c=1)).then_inc(records_ready, 1)

            for n in range(2):
                s = ffn[n]
                if n == 1:
                    with pool.Fori(0, B) as b:
                        for g in range(GROUPS):
                            pool.wait_ge(wide_read, b * WIDE_B + (2 + WIDE_G * g))
                            src = v_raw[:, :, :].rearrange("p k (r a d) -> p k r a d", a=2, d=HD)
                            bias = v_bias[:, :].rearrange("p (r a d) -> p r a d", a=2, d=HD)
                            for k in range(NB):
                                nc.gpsimd.tensor_tensor(
                                    v_pair[:, g, k, :, 0:18].rearrange("p r (a d) -> p r a d", a=2)[:, :, :, 0:HD],
                                    src[:, k], bias, ALU.add).then_inc(v_ready, 1)
                                flat = v_head[:, g, k, :, :, :].rearrange("p r a w -> p r (a w)")
                                for a in range(2):
                                    nc.gpsimd.tensor_tensor(flat[:, :, 41 * a:41 * a + HD], src[:, k, :, a, :],
                                                            bias[:, :, a, :], ALU.add).then_inc(v_ready, 1)

                if n == 0:
                    pool.wait_ge(zeroed, 16 * ZERO_DMAS)
                pool.wait_ge(s.positions, 1)
                pool.wait_ge(s.norm2, NT)
                for t in range(NT):
                    pool.indirect_dma_start(
                        out=sorted_in[:, :], out_offset=bass.IndirectOffsetOnAxis(ap=pos[:, t:t + 1], axis=0),
                        in_=xn[:, t, :], in_offset=None).then_inc(s.scattered, 16)
                if n == 0:
                    pool.wait_ge(experts_loaded, 16 * (2 + FC))
                    pool.wait_ge(records_ready, 3)
                pool.wait_ge(s.table, 1)

                def fetch(i, o):
                    at = pool.value_load(owner[0:1, bass.ds(i + o, 1)], min_val=0, max_val=(E - 1) * REC)
                    if not early(i, o, 4):
                        pool.wait_ge(s.rows_out, i + (o - 3))
                    pool.wait_ge(s.weights, i + (o + 1))
                    flat = records[:, :, :].rearrange("p e r -> p (e r)")[:, B2:]
                    nc.gpsimd.tensor_copy(rec[:, ring(o), B2:REC], flat[:, bass.ds(at, REC - B2)]
                                          ).then_inc(s.vectors, 1)

                for o in range(-1, 4):
                    fetch(1, o)
                with pool.Fori(LOOP_FROM, LOOP_TO - 3, 4) as i:
                    for o in range(4):
                        fetch(i, o)
                for o in range(2):
                    fetch(LOOP_TO, o)

                for o in range(-2, 2):
                    pool.wait_ge(s.rows_stored[ring(o)], ring_value(LOOP_TO, o))
                for t in range(NT):
                    pool.indirect_dma_start(
                        out=mix[:, t, :], out_offset=None, in_=sorted_out[:, :],
                        in_offset=bass.IndirectOffsetOnAxis(ap=pos[:, t:t + 1], axis=0)).then_inc(gathered[t], 16)

        @block.scalar
        def _(act):
            act.dma_start(rows[R_B1:R_B1 + E * FC, :], b1.rearrange("e (c p) -> (e c) p", p=P)
                          ).then_inc(small_loaded, 16)
            act.dma_start(rows[R_G:R_G + E, :], ln_g).then_inc(small_loaded, 16)
            act.dma_start(rows[R_B:R_B + E, :], ln_b).then_inc(small_loaded, 16)
            act.dma_start(rows[R_C:R_C + E, :], centroids).then_inc(small_loaded, 16)
            act.dma_start(rows[R_QB:R_QB + 2, :], qkv_b.rearrange("(a d) -> a d", d=D)[0:2, :]
                          ).then_inc(small_loaded, 16)
            act.dma_start(records[:, :, W1:W1 + F], w1.rearrange("e d f -> d e f")).then_inc(experts_loaded, 16)
            act.dma_start(qkv_sb[:, :], qkv_w).then_inc(attn_loaded, 16)
            act.dma_start(proj_sb[:, :], proj.rearrange("h d m -> (h d) m")).then_inc(attn_loaded, 16)
            for c in range(FC):
                act.dma_start(records[:, :, W2 + c * D:W2 + (c + 1) * D],
                              w2[:, c * P:(c + 1) * P, :].rearrange("e p d -> p e d")).then_inc(experts_loaded, 16)
            act.dma_start(records[:, :, B2:B2 + D],
                          b2.rearrange("(o e) d -> o e d", o=1).broadcast_to([P, E, D])).then_inc(experts_loaded, 16)
            act.dma_start(v_bias[:, :], qkv_b.rearrange("(a d) -> a d", d=D)[2:3, :].broadcast_to([P, D])
                          ).then_inc(attn_loaded, 16)
            act.dma_start(outw_sb[:, :], out_w).then_inc(attn_loaded, 16)
            act.dma_start(out_bias[:, :], out_b.rearrange("(a d) -> a d", a=1).broadcast_to([P, D])
                          ).then_inc(attn_loaded, 16)

            def deviation(out_ap, var_ap, signal):
                nc.scalar.activation(out_ap, var_ap, ACT.Sqrt, bias=eps_col[:, 0:1]).then_inc(signal, 1)

            def blocks(q):
                return slice(q * NB, (q + 1) * NB)

            act.wait_ge(filled, 6)
            for n in range(2):
                s = ffn[n]
                for step in range(NT // NB + 2):
                    if step < NT // NB:
                        act.wait_ge(s.aggr1, AGGR * (step + 1))
                        deviation(dev[:, blocks(step)], mv1[:, 1, blocks(step)], s.dev1)
                    q = step - 1
                    if 0 <= q < NT // NB:
                        act.wait_ge(s.f_turned, q + 1)
                        nc.scalar.activation(f_turned[:, blocks(q), :], psum[:, q % 2, :], ACT.Copy
                                             ).then_inc(s.f_turned_sb, 1)
                        act.wait_ge(s.aggr2, AGGR * (q + 1))
                        deviation(dev_b[:, blocks(q)], mv2[:, 1, blocks(q)], s.dev2)
                if n == 0:
                    act.wait_ge(w_turned_psum, 1)
                    nc.scalar.activation(w_turned[:, :, :], psum[:, 4, 0:2 * P], ACT.Copy).then_inc(w_turned_sb, 1)
                    for j in range(4):
                        act.wait_ge(w_feat_psum, j + 1)
                        nc.scalar.activation(w_feat[:, j // 2, (j % 2) * 512:(j % 2 + 1) * 512],
                                             psum[:, 4 + j, :], ACT.Copy).then_inc(w_feat_sb, 1)
                    act.wait_ge(b_feat_psum, 1)
                    nc.scalar.activation(b_feat[:, :, :], psum[:, 1, 0:2 * PAIRS], ACT.Copy).then_inc(w_feat_sb, 1)
                act.wait_ge(s.route, 1)
                nc.scalar.activation(alpha[:, :], best[:, :], ACT.Sigmoid).then_inc(s.gate, 1)

                def relu(i, o, par):
                    act.wait_ge(s.up, 2 * (i + o) + 1)
                    for c in range(FC // 2):
                        nc.scalar.activation(hid[:, par, c, :], psum[:, 4 + 2 * par, c * P:(c + 1) * P], ACT.Relu,
                                             bias=rec[:, ring(o), B1 + c:B1 + c + 1]).then_inc(s.relu_act, 1)

                def fetch(i, o):
                    at = act.value_load(owner[0:1, bass.ds(i + o, 1)], min_val=0, max_val=(E - 1) * REC)
                    if not early(i, o, 4):
                        act.wait_ge(s.down, i + (o - 3))
                    flat = records[:, :, :].rearrange("p e r -> p (e r)")
                    nc.scalar.activation(rec[:, ring(o), W1:B2], flat[:, bass.ds(at, B2 - W1)], ACT.Copy
                                         ).then_inc(s.weights, 1)

                if n == 0:
                    act.wait_ge(experts_loaded, 16 * (2 + FC))
                act.wait_ge(s.table, 1)
                for o in range(-1, 1):
                    fetch(1, o)
                for o in range(-1, 4):
                    fetch(1, o + 2)
                    relu(1, o, (1 + o) % 2)
                with act.Fori(LOOP_FROM, LOOP_TO - 3, 4) as i:
                    for o in range(4):
                        fetch(i, o + 2)
                        relu(i, o, (1 + o) % 2)
                for o in range(2):
                    relu(LOOP_TO, o, (1 + o) % 2)

                if n == 1:
                    continue
                act.wait_ge(a_aggr, AGGR)
                deviation(dev[:, 0:NB], mv1[:, 1, 0:NB], a_dev)
                act.wait_ge(wide_done, 1)
                nc.scalar.activation(xaT[:, :, :], psum[:, 0, :], ACT.Copy).then_inc(wide_read, 1)

                def keys_rows(b, g, k):
                    if (g, k) != (0, 0):
                        act.wait_ge(stateT_done, b * (CHUNKS - 1) + (NB * g + k))
                    for h in range(2):
                        idx = KEY_ROWS + 2 * k + h
                        act.wait_ge(wide_done, wide(b, g, idx) + 1)
                        nc.scalar.activation(k_rows[:, 4 * h:4 * h + 4, :], psum[:, (1 + idx) % 2, :], ACT.Copy
                                             ).then_inc(wide_read, 1)

                def heads_turn(b, c):
                    act.wait_ge(heads_turned, b * CHUNKS + (c + 1))
                    nc.scalar.activation(heads_T[:, :], psum[:, 6, 0:P], ACT.Copy).then_inc(heads_T_ready, 1)

                act.wait_ge(w_feat_sb, 5)
                with act.Fori(0, B) as b:
                    for g in range(GROUPS):
                        act.wait_ge(wide_done, wide(b, g, 0) + 1)
                        nc.scalar.activation(v_raw[:, :, :], psum[:, 1, :], ACT.Copy).then_inc(wide_read, 1)
                        for r in range(PAIRS):
                            for a, dst in ((0, qT), (1, kT)):
                                idx = 1 + 2 * r + a
                                act.wait_ge(wide_done, wide(b, g, idx) + 1)
                                nc.scalar.activation(dst[:, r, :], psum[:, (1 + idx) % 2, :], ACT.Relu,
                                                     bias=b_feat[:, r, a:a + 1]).then_inc(wide_read, 1)
                                if g == 1 and idx == 6:
                                    heads_turn(b, NB * g - 1)
                        for k in range(NB):
                            c = NB * g + k
                            if c < CHUNKS - 1:
                                keys_rows(b, g, k)
                            if k == NB - 1:
                                idx = turn_idx(g)
                                act.wait_ge(wide_done, wide(b, g, idx) + 1)
                                nc.scalar.activation(xaT[:, :, :], psum[:, (1 + idx) % 2, :], ACT.Copy
                                                     ).then_inc(wide_read, 1)
                            act.wait_ge(o_done, b * CHUNKS + (c + 1))
                            nc.scalar.activation(o_sb[:, :, :], psum[:, 6, 0:2 * P], ACT.Copy).then_inc(o_read, 1)
                            if k == 1:
                                act.wait_ge(a_aggr, b * (AGGR * GROUPS) + AGGR * (g + 2))
                                deviation(dev[:, 0:NB], mv1[:, 1, 0:NB], a_dev)
                            if k < NB - 1 or g == GROUPS - 1:
                                heads_turn(b, c)

        @block.tensor
        def _(pe):
            def turn(bank, at, src):
                return nc.tensor.transpose(psum[:, bank, at:at + src.shape[0]], src, ident[0:src.shape[0], 0:src.shape[0]])

            pe.wait_ge(consts, 1)
            pe.wait_ge(small_loaded, 80)
            nc.tensor.transpose(psum[:, 3, 0:NR], rows[:, :], ident[0:NR, 0:NR]).then_inc(cols_psum, 1)

            for n in range(2):
                s = ffn[n]
                for q in range(NT // NB + 1):
                    if q < NT // NB:
                        pe.wait_ge(s.norm1, NB * (q + 1))
                        if q >= 2:
                            pe.wait_ge(s.f_turned_sb, q - 1)
                        for t in range(NB):
                            last = turn(q % 2, t * P, f[:, q * NB + t, :])
                        last.then_inc(s.f_turned, 1)
                    if q > 0:
                        pe.wait_ge(s.f_turned_sb, q)
                        if n == 0 and q == 1:
                            pe.wait_ge(cols_ready, 1)
                        for t in range((q - 1) * NB, q * NB):
                            last = nc.tensor.matmul(psum[:, 2, t * E:(t + 1) * E], f_turned[:, t, :],
                                                    cols[:, R_C:R_C + E], start=True, stop=True)
                last.then_inc(s.affinity, 1)
                if n == 0:
                    pe.wait_ge(attn_loaded, 80)
                    for a in range(2):
                        last = turn(4, a * P, qkv_sb[:, a * D:(a + 1) * D])
                    last.then_inc(w_turned_psum, 1)
                    pe.wait_ge(w_turned_sb, 1)
                    pe.wait_ge(wide_ready, 1)
                    wide_flat = proj_wide[:, :, :].rearrange("p h m -> p (h m)")
                    for j in range(4):
                        nc.tensor.matmul(psum[:, 4 + j, :], w_turned[:, j // 2, :],
                                         wide_flat[:, (j % 2) * 512:(j % 2 + 1) * 512], start=True, stop=True
                                         ).then_inc(w_feat_psum, 1)
                    for r in range(PAIRS):
                        last = nc.tensor.matmul(psum[:, 1, 2 * r:2 * r + 2], wide_flat[:, r * P:(r + 1) * P],
                                                cols[:, R_QB:R_QB + 2], start=True, stop=True)
                    last.then_inc(b_feat_psum, 1)
                if n == 0:
                    pe.wait_ge(consts, 8)
                pe.wait_ge(s.onehot, 1)
                hot = onehot[:, :, :].rearrange("p e t -> p (e t)")
                nc.tensor.matmul(psum[:, 3, 0:E * NT], before[:, :], hot, start=True, stop=True)
                nc.tensor.matmul(psum[:, 3, E * NT:2 * E * NT], ones[:, :], hot, start=True, stop=True
                                 ).then_inc(s.counts, 1)

                def turn_rows(i, o, par):
                    pe.wait_ge(s.rows_loaded[ring(o)], ring_value(i, o))
                    turn(par, 0, rows_in[:, ring(o), :]).then_inc(s.rows_turned, 1)

                def up(i, o, par):
                    pe.wait_ge(s.inputs, i + (o + 1))
                    for c in range(FC):
                        last = nc.tensor.matmul(psum[:, 4 + 2 * par + c // 2, (c % 2) * P:(c % 2 + 1) * P],
                                                rec[:, ring(o), W1 + c * P:W1 + (c + 1) * P], lnT[:, par, :],
                                                start=True, stop=True)
                        if c % 2:
                            last.then_inc(s.up, 1)

                def down(i, o, par):
                    pe.wait_ge(s.relu_act, 2 * (i + o) + 2)
                    pe.wait_ge(s.relu_dve, 2 * (i + o) + 2)
                    for c in range(FC):
                        last = nc.tensor.matmul(psum[:, 2 + par, 0:D], hid[:, par, c, :],
                                                rec[:, ring(o), W2 + c * D:W2 + (c + 1) * D],
                                                start=(c == 0), stop=(c == FC - 1))
                    last.then_inc(s.down, 1)

                def tile_step(i, o):
                    up(i, o, (1 + o) % 2)
                    if not (isinstance(i, int) and i + o == NS - 1):
                        turn_rows(i, o + 1, o % 2)
                    if not early(i, o, 1):
                        down(i, o - 1, o % 2)

                pe.wait_ge(s.positions, 1)
                if n == 0:
                    pe.wait_ge(w_feat_sb, 5)
                turn_rows(1, -1, 0)
                for o in range(-1, 4):
                    tile_step(1, o)
                with pe.Fori(LOOP_FROM, LOOP_TO - 3, 4) as i:
                    for o in range(4):
                        tile_step(i, o)
                for o in range(2):
                    tile_step(LOOP_TO, o)
                down(LOOP_TO, 1, 0)

                if n == 1:
                    continue
                pe.wait_ge(a_norm, NB)
                for t in range(NB):
                    last = turn(0, t * P, xa[:, t, :])
                last.then_inc(wide_done, 1)

                def values(b, g):
                    pe.wait_ge(wide_read, wide(b, g, 0))
                    for k in range(NB):
                        last = nc.tensor.matmul(psum[:, 1, k * P:(k + 1) * P], xaT[:, k, :], qkv_sb[:, 2 * D:3 * D],
                                                start=True, stop=True)
                    last.then_inc(wide_done, 1)

                def features(b, g, r):
                    for a in range(2):
                        idx = 1 + 2 * r + a
                        pe.wait_ge(wide_read, wide(b, g, idx) - 1)
                        nc.tensor.matmul(psum[:, (1 + idx) % 2, :], w_feat[:, a, r * P:(r + 1) * P],
                                         xaT[:, :, :].rearrange("p k t -> p (k t)"), start=True, stop=True
                                         ).then_inc(wide_done, 1)

                def score(g, k, half):
                    at = slice(k * P, (k + 1) * P)
                    for r in range(4):
                        for a in range(2):
                            last = nc.tensor.matmul(psum[:, 2 + 2 * half + a, r * P:(r + 1) * P],
                                                    kT[64 * a:64 * a + 64, 4 * half + r, at],
                                                    qT[64 * a:64 * a + 64, 4 * half + r, at], start=True, stop=True)
                            if r == 3:
                                last.then_inc(scored, 1)

                def key_rows(b, g, k):
                    for h in range(2):
                        idx = KEY_ROWS + 2 * k + h
                        pe.wait_ge(wide_read, wide(b, g, idx) - 1)
                        for r in range(4):
                            last = turn((1 + idx) % 2, r * P, kT[:, 4 * h + r, k * P:(k + 1) * P])
                        last.then_inc(wide_done, 1)

                def turn_next(b, g):
                    idx = turn_idx(g)
                    pe.wait_ge(wide_read, wide(b, g, idx) - 1)
                    pe.wait_ge(a_norm, b * (NB * GROUPS) + NB * (g + 2))
                    for t in range(NB):
                        last = turn((1 + idx) % 2, t * P, xa[:, t, :])
                    last.then_inc(wide_done, 1)

                def context(b, g, k):
                    c = NB * g + k
                    pe.wait_ge(state_ready, b * CHUNKS + (c + 1))
                    if c > 0:
                        pe.wait_ge(projected_sb, b * CHUNKS + c)
                    for half in range(2):
                        for r in range(4):
                            nc.tensor.matmul(psum[32 * r:32 * r + 32, 6, half * P:(half + 1) * P],
                                             state[:, 4 * half + r, :], qT[:, 4 * half + r, k * P:(k + 1) * P],
                                             start=(half == 0), stop=False, skip_group_check=True)
                    if k == 0:
                        pe.wait_ge(v_ready, b * (3 * CHUNKS) + 3 * NB * (g + 1))
                    for half in range(2):
                        for a in range(2):
                            pe.wait_ge(masked, b * (4 * CHUNKS) + (4 * c + 2 * half + a + 1))
                            for r in range(4):
                                last = nc.tensor.matmul(psum[32 * r:32 * r + 32, 6, half * P:(half + 1) * P],
                                                        v_head[:, g, k, 4 * half + r, a, :],
                                                        scores[:, k % 2, 2 * half + a, r, :],
                                                        start=False, stop=(half == 1 and a == 1),
                                                        skip_group_check=True)
                    last.then_inc(o_done, 1)

                def turn_context(b, c):
                    pe.wait_ge(o_read, b * CHUNKS + (c + 1))
                    for half in range(2):
                        last = turn(6, half * P, o_sb[:, half, :])
                    last.then_inc(o_turned, 1)

                def state_sums(b, g, k):
                    pe.wait_ge(wide_read, wide(b, g, KEY_ROWS + 2 * k + 1) + 1)
                    for half in range(2):
                        for r in range(4):
                            last = nc.tensor.matmul(psum[32 * r:32 * r + 32, 7, half * P:(half + 1) * P],
                                                    v_pair[:, g, k, 4 * half + r, :], k_rows[:, 4 * half + r, :],
                                                    start=True, stop=True)
                    last.then_inc(stateT_done, 1)

                def turn_state(b, c):
                    pe.wait_ge(stateT_added, b * (CHUNKS - 1) + (c + 1))
                    for half in range(2):
                        last = turn(7, half * P, stateT[:, half, :])
                    last.then_inc(state_turned, 1)

                def turn_heads(b, c):
                    pe.wait_ge(heads_ready, b * CHUNKS + (c + 1))
                    turn(6, 0, heads_out[:, :, :, :].rearrange("p r a d -> p (r a d)")).then_inc(heads_turned, 1)

                def project(b, c):
                    pe.wait_ge(heads_T_ready, b * CHUNKS + (c + 1))
                    nc.tensor.matmul(psum[:, 6, 0:D], heads_T[:, :], outw_sb[:, :], start=True, stop=True
                                     ).then_inc(projected, 1)

                with pe.Fori(0, B) as b:
                    for g in range(GROUPS):
                        values(b, g)
                        for r in range(PAIRS):
                            features(b, g, r)
                            if g > 0:
                                if r == 0:
                                    turn_context(b, NB * g - 1)
                                    state_sums(b, g - 1, NB - 1)
                                if r == 1:
                                    turn_heads(b, NB * g - 1)
                                    turn_state(b, NB * g - 1)
                                if r == 4:
                                    project(b, NB * g - 1)
                        pe.wait_ge(wide_read, wide(b, g, 2 * PAIRS) + 1)
                        for half in range(2):
                            score(g, 0, half)
                        for k in range(NB):
                            c = NB * g + k
                            if c < CHUNKS - 1:
                                key_rows(b, g, k)
                            if k == NB - 1:
                                turn_next(b, g)
                            context(b, g, k)
                            if k < NB - 1:
                                score(g, k + 1, 0)
                                turn_context(b, c)
                                state_sums(b, g, k)
                                score(g, k + 1, 1)
                                turn_heads(b, c)
                                turn_state(b, c)
                                project(b, c)
                            elif g == GROUPS - 1:
                                turn_context(b, c)
                                turn_heads(b, c)
                                project(b, c)

        @block.vector
        def _(dve):
            def norm_stats(tiles, source, stats_to, mv, stats_signal, aggr_signal, blocks_before):
                for k, t in enumerate(tiles):
                    nc.vector.bn_stats(stats_to[:, t, :], source(k)).then_inc(stats_signal, 1)
                q = slice(tiles[0], tiles[0] + NB)
                steps = blocks_before * AGGR
                dve.wait_ge(stats_signal, (blocks_before + 1) * NB)
                nc.vector.tensor_tensor(halves[:, 0, :], stats_to[:, q, 1], stats_to[:, q, 4], ALU.add
                                        ).then_inc(aggr_signal, 1)
                nc.vector.tensor_tensor(halves[:, 1, :], stats_to[:, q, 1], stats_to[:, q, 4], ALU.subtract
                                        ).then_inc(aggr_signal, 1)
                nc.vector.tensor_tensor(halves[:, 2, :], stats_to[:, q, 2], stats_to[:, q, 5], ALU.add
                                        ).then_inc(aggr_signal, 1)
                dve.wait_ge(aggr_signal, steps + 3)
                nc.vector.scalar_tensor_tensor(out=halves[:, 3, :], in0=halves[:, 1, :], scalar=0.25,
                                               in1=halves[:, 1, :], op0=ALU.mult, op1=ALU.mult
                                               ).then_inc(aggr_signal, 1)
                nc.vector.tensor_scalar(mv[:, 0, q], halves[:, 0, :], 0.5, None, ALU.mult).then_inc(aggr_signal, 1)
                dve.wait_ge(aggr_signal, steps + 5)
                nc.vector.scalar_tensor_tensor(out=mv[:, 1, q], in0=halves[:, 2, :], scalar=1.0 / D,
                                               in1=halves[:, 3, :], op0=ALU.mult, op1=ALU.add
                                               ).then_inc(aggr_signal, 1)

            def norm_apply(tiles, source, dest, mv, dev_, rstd_, dev_signal, rstd_signal, norm_signal, blocks_before):
                dve.wait_ge(dev_signal, blocks_before + 1)
                nc.vector.reciprocal(rstd_[:, tiles[0]:tiles[0] + NB], dev_[:, tiles[0]:tiles[0] + NB]
                                     ).then_inc(rstd_signal, 1)
                dve.wait_ge(rstd_signal, blocks_before + 1)
                for k, t in enumerate(tiles):
                    nc.vector.tensor_scalar(dest(k), source(k), mv[:, 0, t:t + 1], rstd_[:, t:t + 1],
                                            ALU.subtract, ALU.mult).then_inc(norm_signal, 1)

            for n in range(2):
                s = ffn[n]
                if n == 1:
                    dve.wait_ge(residual, NT)
                for step in range(NT // NB + 2):
                    if step < NT // NB:
                        q = step
                        ts_ = list(range(q * NB, (q + 1) * NB))
                        if n == 0:
                            dve.wait_ge(x_loaded[q], 16)
                        norm_stats(ts_, lambda k: x[:, q * NB + k, :], stats, mv1, s.stats1, s.aggr1, q)
                    if n == 0 and step == 0:
                        dve.wait_ge(cols_psum, 1)
                        nc.vector.tensor_copy(cols[:, :], psum[:, 3, 0:NR]).then_inc(cols_ready, 1)
                    q = step - 1
                    if 0 <= q < NT // NB:
                        ts_ = list(range(q * NB, (q + 1) * NB))
                        norm_apply(ts_, lambda k: x[:, q * NB + k, :], lambda k: f[:, q * NB + k, :], mv1, dev, rstd,
                                   s.dev1, s.rstd1, s.norm1, q)
                        dve.wait_ge(s.norm1, NB * (q + 1))
                        norm_stats(ts_, lambda k: f[:, q * NB + k, :], stats_b, mv2, s.stats2, s.aggr2, q)
                    q = step - 2
                    if 0 <= q < NT // NB:
                        ts_ = list(range(q * NB, (q + 1) * NB))
                        norm_apply(ts_, lambda k: f[:, q * NB + k, :], lambda k: xn[:, q * NB + k, :], mv2, dev_b,
                                   rstd_b, s.dev2, s.rstd2, s.norm2, q)

                route = [0]

                def link(ins):
                    route[0] += 1
                    ins.then_inc(s.route, 1)
                    dve.wait_ge(s.route, route[0])

                def over_t(ap, width):
                    return ap.unsqueeze(2).broadcast_to([P, ap.shape[1], width])

                def over_first(ap, count):
                    return ap.unsqueeze(1).broadcast_to([P, count, ap.shape[1]])

                dve.wait_ge(s.affinity, 1)
                if n == 0:
                    dve.wait_ge(consts, 8)
                aff = psum[:, 2, 0:NT * E].rearrange("p (t e) -> p t e", e=E)
                link(nc.vector.reduce_max(best[:, :], aff, AX_X))
                link(nc.vector.tensor_tensor(is_best[:, :, :], aff, over_t(best[:, :], E), ALU.is_ge))
                link(nc.vector.tensor_tensor(ranked[:, :, :], is_best[:, :, :], over_first(first_rank[:, :], NT), ALU.mult))
                link(nc.vector.reduce_max(best_rank[:, :], ranked[:, :, :], AX_X))
                nc.vector.tensor_tensor(onehot[:, :, :].rearrange("p e t -> p t e"), ranked[:, :, :],
                                        over_t(best_rank[:, :], E), ALU.is_equal).then_inc(s.onehot, 1)
                if n == 0:
                    dve.wait_ge(attn_loaded, 80)
                    nc.vector.tensor_tensor(proj_wide[:, :, :], over_first(proj_sb[:, :], H),
                                            over_t(head_block[:, :], M), ALU.mult).then_inc(wide_ready, 1)
                dve.wait_ge(s.counts, 1)
                dve.wait_ge(s.onehot, 1)
                tot = psum[:, 3, E * NT:2 * E * NT]
                tot3 = tot.rearrange("p (e t) -> p e t", t=NT)
                pre3 = psum[:, 3, 0:E * NT].rearrange("p (e t) -> p e t", t=NT)
                link(nc.vector.reduce_sum(n_e[:, :], tot3, AX_X))
                link(nc.vector.tensor_tensor(over[:, :, :], over_t(n_e[:, :], NT), over_first(tile_edges[:, :], E), ALU.is_gt))
                link(nc.vector.reduce_sum(tiles_e[:, :], over[:, :, :], AX_X))
                link(nc.vector.tensor_tensor_scan(tiles_upto[:, :], ones[:, 0:E], tiles_e[:, :], 0.0, ALU.mult, ALU.add))
                link(nc.vector.tensor_tensor_scan(run_incl[:, :], ones[:, 0:E * NT], tot, 0.0, ALU.mult, ALU.add))
                link(nc.vector.tensor_tensor(run_excl[:, :, :].rearrange("p e t -> p (e t)"), run_incl[:, :], tot, ALU.subtract))
                link(nc.vector.tensor_tensor(start_e[:, :], tiles_upto[:, :], tiles_e[:, :], ALU.subtract))
                link(nc.vector.scalar_tensor_tensor(out=shift_e[:, :], in0=start_e[:, :], scalar=float(P),
                                                    in1=run_excl[:, :, 0], op0=ALU.mult, op1=ALU.subtract))
                link(nc.vector.tensor_tensor(offset[:, :, :], run_excl[:, :, :], over_t(shift_e[:, :], NT), ALU.add))
                link(nc.vector.tensor_tensor(rank_at[:, :, :], pre3, offset[:, :, :], ALU.add))
                link(nc.vector.tensor_tensor(chosen_at[:, :, :], rank_at[:, :, :], onehot[:, :, :], ALU.mult))
                link(nc.vector.reduce_sum(pos_f[:, :], chosen_at[:, :, :].rearrange("p e t -> p t e"), AX_X))
                nc.vector.tensor_copy(pos[:, :], pos_f[:, :]).then_inc(s.positions, 1)
                link(nc.vector.tensor_tensor(passed[:, :, :], over_t(slots[:, :], E), over_first(tiles_upto[:, :], NS + 1), ALU.is_ge))
                link(nc.vector.reduce_sum(owner_f[:, :], passed[:, :, :], AX_X))
                link(nc.vector.tensor_scalar(owner_at[:, :], owner_f[:, :], float(E - 1), float(REC), ALU.min, ALU.mult))
                nc.vector.tensor_copy(owner[:, :], owner_at[:, :]).then_inc(s.table, 1)

                def scaled(i, o, par):
                    dve.wait_ge(s.rows_turned, i + (o + 1))
                    dve.wait_ge(s.vectors, i + (o + 1))
                    nc.vector.tensor_scalar(lnT[:, par, :], psum[:, par, 0:P], rec[:, ring(o), GG:GG + 1],
                                            rec[:, ring(o), BB:BB + 1], ALU.mult, ALU.add).then_inc(s.inputs, 1)

                def relu(i, o, par):
                    dve.wait_ge(s.up, 2 * (i + o) + 2)
                    for c in range(FC // 2, FC):
                        nc.vector.tensor_scalar(hid[:, par, c, :], psum[:, 5 + 2 * par, (c - 2) * P:(c - 1) * P],
                                                rec[:, ring(o), B1 + c:B1 + c + 1], 0.0, ALU.add, ALU.max
                                                ).then_inc(s.relu_dve, 1)

                def result(i, o, par):
                    dve.wait_ge(s.down, i + (o + 1))
                    if not early(i, o, 4):
                        dve.wait_ge(s.rows_stored[ring(o)], ring_value(i, o - 4))
                    nc.vector.tensor_tensor(rows_out[:, ring(o), :], psum[:, 2 + par, 0:D],
                                            rec[:, ring(o), B2:B2 + D], ALU.add).then_inc(s.rows_out, 1)

                def tile_step(i, o):
                    if not (isinstance(i, int) and i + o == NS - 1):
                        scaled(i, o + 1, o % 2)
                    relu(i, o, (1 + o) % 2)
                    if not early(i, o, 1):
                        result(i, o - 1, o % 2)

                scaled(1, -1, 0)
                for o in range(-1, 4):
                    tile_step(1, o)
                with dve.Fori(LOOP_FROM, LOOP_TO - 3, 4) as i:
                    for o in range(4):
                        tile_step(i, o)
                for o in range(2):
                    tile_step(LOOP_TO, o)
                result(LOOP_TO, 1, 0)

                dve.wait_ge(s.gate, 1)
                for t in range(NT):
                    dve.wait_ge(gathered[t], 16 * (n + 1))
                    nc.vector.scalar_tensor_tensor(out=mix[:, t, :], in0=mix[:, t, :], scalar=alpha[:, t:t + 1],
                                                   in1=f[:, t, :], op0=ALU.mult, op1=ALU.add).then_inc(s.mixed, 1)
                    dve.wait_ge(s.mixed, t + 1)
                    nc.vector.scalar_tensor_tensor(out=x[:, t, :], in0=mix[:, t, :], scalar=0.5,
                                                   in1=x[:, t, :], op0=ALU.mult, op1=ALU.add).then_inc(s.result, 1)
                if n == 1:
                    continue

                dve.wait_ge(s.result, NT)
                dve.wait_ge(filled, 9)
                dve.wait_ge(consts, 8)
                norm_stats(list(range(NB)), lambda k: x[:, k, :], stats, mv1, a_stats, a_aggr, 0)
                norm_apply(list(range(NB)), lambda k: x[:, k, :], lambda k: xa[:, k, :], mv1, dev, rstd,
                           a_dev, a_rstd, a_norm, 0)

                def mask(b, c, quad):
                    dve.wait_ge(scored, b * (4 * CHUNKS) + (4 * c + quad + 1))
                    nc.vector.tensor_tensor(scores[:, c % 2, quad, :, :],
                                            psum[:, 2 + quad, :].rearrange("p (r t) -> p r t", t=P),
                                            over_first(causal[:, :], NB), ALU.mult).then_inc(masked, 1)

                ctx4 = psum[:, 6, 0:2 * P].rearrange("p (r w) -> p r w", w=32)[:, :, 0:18].rearrange(
                    "p r (a w) -> p r a w", a=2)

                def divide(b, c):
                    dve.wait_ge(o_turned, b * CHUNKS + (c + 1))
                    nc.vector.tensor_scalar(den[:, :, :].unsqueeze(3), ctx4[:, :, :, HD:HD + 1], DEN_EPS, None,
                                            ALU.add).then_inc(den_ready, 1)
                    dve.wait_ge(den_ready, b * CHUNKS + (c + 1))
                    nc.vector.reciprocal(inv_den[:, :, :], den[:, :, :]).then_inc(inv_ready, 1)
                    dve.wait_ge(inv_ready, b * CHUNKS + (c + 1))
                    nc.vector.tensor_tensor(heads_out[:, :, :, :], ctx4[:, :, :, 0:HD],
                                            inv_den[:, :, :].unsqueeze(3).broadcast_to([P, PAIRS, 2, HD]),
                                            ALU.mult).then_inc(heads_ready, 1)

                def add_state(b, c):
                    dve.wait_ge(stateT_done, b * (CHUNKS - 1) + (c + 1))
                    sums = psum[:, 7, 0:2 * P].rearrange("p (h m) -> p h m", m=P)
                    if c == 0:
                        nc.vector.tensor_copy(stateT[:, :, :], sums).then_inc(stateT_added, 1)
                    else:
                        dve.wait_ge(stateT_added, b * (CHUNKS - 1) + c)
                        nc.vector.tensor_tensor(stateT[:, :, :], sums, stateT[:, :, :], ALU.add
                                                ).then_inc(stateT_added, 1)

                def split_state(b, c):
                    dve.wait_ge(state_turned, b * (CHUNKS - 1) + (c + 1))
                    dve.wait_ge(state_ready, b * CHUNKS + (c + 1))
                    turned = psum[:, 7, 0:2 * P].rearrange("p (r w) -> p r w", w=32)
                    nc.vector.tensor_copy(state[0:64, :, 0:9], turned[0:64, :, 0:9])
                    nc.vector.tensor_copy(state[64:P, :, 9:18], turned[64:P, :, 9:18]).then_inc(state_ready, 1)

                def add_out(b, c):
                    dve.wait_ge(projected, b * CHUNKS + (c + 1))
                    if c > 0:
                        dve.wait_ge(residual, b * CHUNKS + c)
                    nc.vector.tensor_tensor(proj_out[:, :], psum[:, 6, 0:D], out_bias[:, :], ALU.add
                                            ).then_inc(projected_sb, 1)
                    dve.wait_ge(projected_sb, b * CHUNKS + (c + 1))
                    at = bass.ds(b * CHUNKS + c, 1)
                    nc.vector.tensor_tensor(x[:, at, :], x[:, at, :], proj_out[:, :].unsqueeze(1), ALU.add
                                            ).then_inc(residual, 1)

                with dve.Fori(0, B) as b:
                    nc.vector.memset(state[:, :, :], 0.0).then_inc(state_ready, 1)
                    for g in range(GROUPS):
                        done = NB * g - 1
                        if g > 0:
                            divide(b, done)
                            add_state(b, done)
                            split_state(b, done)
                            add_out(b, done)
                        for quad in range(4):
                            mask(b, NB * g, quad)
                        blocks = b * GROUPS + (g + 1)
                        for k in range(NB):
                            c = NB * g + k
                            source = lambda j: x[:, bass.ds(blocks * NB + j, 1), :].squeeze(1)
                            if k == 0:
                                norm_stats(list(range(NB)), source, stats, mv1, a_stats, a_aggr, blocks)
                            if k == 1:
                                norm_apply(list(range(NB)), source, lambda j: xa[:, j, :], mv1, dev, rstd,
                                           a_dev, a_rstd, a_norm, blocks)
                            if k < NB - 1:
                                mask(b, c + 1, 0)
                                mask(b, c + 1, 1)
                                divide(b, c)
                                add_state(b, c)
                                mask(b, c + 1, 2)
                                mask(b, c + 1, 3)
                                split_state(b, c)
                                add_out(b, c)
                            elif g == GROUPS - 1:
                                divide(b, c)
                                add_out(b, c)
                    dve.wait_ge(residual, b * CHUNKS + CHUNKS)


_ORDER = ["L0_attn_x", "L0_attn_qkv_w", "L0_attn_qkv_b", "L0_attn_out_w", "L0_attn_out_b", "L0_attn_proj",
          "L0_ffn_centroids", "L0_ffn_ln_g", "L0_ffn_ln_b", "L0_ffn_w1", "L0_ffn_b1", "L0_ffn_w2", "L0_ffn_b2"]


def kernel(**inputs):
    import numpy as _np
    import concourse.bacc as _bacc
    from concourse import mybir as _mybir
    from concourse.bass_utils import run_bass_kernel_spmd as _run

    nc = _bacc.Bacc("TRN2", target_bir_lowering=False, num_devices=1)
    arrays, args = {}, []
    for name in _ORDER:
        a = _np.ascontiguousarray(inputs[name])
        arrays[f"in_{name}"] = a
        args.append(nc.dram_tensor(f"in_{name}", a.shape, _mybir.dt.from_np(a.dtype), kind="ExternalInput").ap())
    shape = tuple(inputs["L0_attn_x"].shape)
    out = nc.dram_tensor("out_x", shape, F32, kind="ExternalOutput").ap()
    macaron_block(nc, *args, out)
    r = _run(nc, [arrays], core_ids=[0])
    return r.results[0]["out_x"]
```

```python
from contextlib import ExitStack

import concourse.bass as bass
from concourse import mybir

P = 128
F32 = mybir.dt.float32
I32 = mybir.dt.int32
BF16 = mybir.dt.bfloat16
ALU = mybir.AluOpType
ACT = mybir.ActivationFunctionType
AX_X = mybir.AxisListType.X
LN_EPS = 1e-5
DEN_EPS = 1e-6


class FfnSignals:

    def __init__(self, sem, n):
        self.stats1 = sem(f"stats1_{n}")
        self.aggr1 = sem(f"aggr1_{n}")
        self.dev1 = sem(f"dev1_{n}")
        self.rstd1 = sem(f"rstd1_{n}")
        self.norm1 = sem(f"norm1_{n}")
        self.var2 = sem(f"var2_{n}")
        self.dev2 = sem(f"dev2_{n}")
        self.rstd2 = sem(f"rstd2_{n}")
        self.norm2 = sem(f"norm2_{n}")
        self.xn_stored = sem(f"xn_stored_{n}")
        self.f_turned = sem(f"f_turned_{n}")
        self.f_turned_sb = sem(f"f_turned_sb_{n}")
        self.affinity = sem(f"affinity_{n}")
        self.gate = sem(f"gate_{n}")
        self.route = sem(f"route_{n}")
        self.onehot = sem(f"onehot_{n}")
        self.counts = sem(f"counts_{n}")
        self.table = sem(f"table_{n}")
        self.place_hot = sem(f"place_hot_{n}")
        self.inverse = sem(f"inverse_{n}")
        self.sources = sem(f"sources_{n}")
        self.targets = sem(f"targets_{n}")
        self.weights = sem(f"weights_{n}")
        self.rows_turned = sem(f"rows_turned_{n}")
        self.inputs = sem(f"inputs_{n}")
        self.up = sem(f"up_{n}")
        self.relu_act = sem(f"relu_act_{n}")
        self.relu_dve = sem(f"relu_dve_{n}")
        self.down = sem(f"down_{n}")
        self.rows_out = sem(f"rows_out_{n}")
        self.halved = sem(f"halved_{n}")
        self.result = sem(f"result_{n}")
        self.rows_loaded = [sem(f"rows_loaded{r}_{n}") for r in range(4)]
        self.rows_stored = [sem(f"rows_stored{r}_{n}") for r in range(4)]
        self.mix_loaded = [sem(f"mix_loaded{q}_{n}") for q in range(4)]


def macaron_block(nc, x_in, qkv_w, qkv_b, out_w, out_b, proj, centroids, ln_g, ln_b, w1, b1, w2, b2, out):
    B, L, D = x_in.shape
    H, HD, M = proj.shape
    E, _, F = w1.shape
    NT = B * L // P
    FC = F // P
    NS = (B * L + E * (P - 1)) // P
    NB = 4
    PAIRS = H // 2
    CHUNKS = L // P
    GROUPS = CHUNKS // NB
    assert D == P and F == 4 * P and H * HD == P and 2 * M == P and B * L % P == 0 and GROUPS == 2 and PAIRS == 8
    assert NS % 4 == 3
    assert NT // NB == 4

    AGGR = 6

    W1, W2, B2, B1, GG, BB = 0, F, F + FC * P, F + FC * P + D, F + FC * P + D + FC, F + FC * P + D + FC + 1
    REC = BB + 1
    R_B1, R_G, R_B, R_C, R_QB, NR = 0, E * FC, E * FC + E, E * FC + 2 * E, E * FC + 3 * E, E * FC + 3 * E + 2

    xn_rows = nc.dram_tensor("xn_rows", [NT * P, D], F32, kind="Internal").ap()
    ffn_rows = nc.dram_tensor("ffn_rows", [(NT + NS) * P, D], F32, kind="Internal").ap()

    ctx = ExitStack()
    with ctx:
        def sb(name, shape, dt=F32):
            return ctx.enter_context(nc.sbuf_tensor(name, shape, dt))

        def sem(name):
            return ctx.enter_context(nc.semaphore(name))

        psum = ctx.enter_context(nc.psum_tensor("psum", [P, 8, 512], F32))

        ident = sb("ident", [P, P])
        causal = sb("causal", [P, P])
        ones = sb("ones", [P, P])
        later = sb("later", [P, P])
        go_on = sb("go_on", [P, E, NT])
        head_block = sb("head_block", [P, H])
        first_rank = sb("first_rank", [P, E])
        tile_edges = sb("tile_edges", [P, NT])
        slots = sb("slots", [P, NS + 1])
        eps_col = sb("eps_col", [P, 1])
        warm = sb("warm", [P, 1])
        places = sb("places", [P, P])
        partition = sb("partition", [P, 1])
        spare_row = sb("spare_row", [P, NS + 1])
        rows = sb("rows", [NR, P])
        cols = sb("cols", [P, NR])
        records = sb("records", [P, E, REC])
        qkv_sb = sb("qkv_sb", [P, 3 * D])
        v_bias = sb("v_bias", [P, D])
        outw_sb = sb("outw_sb", [P, D])
        out_bias = sb("out_bias", [P, D])
        proj_sb = sb("proj_sb", [P, M])
        w_turned = sb("w_turned", [P, 2, P])
        w_feat = sb("w_feat", [P, 2, H * M])
        b_feat = sb("b_feat", [P, PAIRS, 2])

        x_all = sb("x", [P, NB + NT + NB, D])
        x = x_all[:, NB:NB + NT, :]
        f_all = sb("f", [P, NB + NT, D])
        f = f_all[:, NB:NB + NT, :]
        xn = sb("xn", [P, NT, D])
        mix = xn
        stats = sb("stats", [P, NT, 6])
        mv1 = sb("mv1", [P, 2, NT])
        halves = sb("halves", [P, 4, NB])
        stats_a = sb("stats_a", [P, NB, 6])
        mv_a = sb("mv_a", [P, 2, NB])
        dev_a = sb("dev_a", [P, NB])
        rstd_a = sb("rstd_a", [P, NB])
        stats_f = sb("stats_f", [P, NB, 6])
        mv_f = sb("mv_f", [P, 2, NB])
        dev_f = sb("dev_f", [P, NB])
        rstd_f = sb("rstd_f", [P, NB])
        shrunk_f = sb("shrunk_f", [P, NB])
        dev = sb("dev", [P, NT])
        rstd = sb("rstd", [P, NT])
        shrunk = sb("shrunk", [P, NT])
        var_b = sb("var_b", [P, NB + NT])
        dev_b = sb("dev_b", [P, NT])
        rstd_b = sb("rstd_b", [P, NT])
        best = sb("best", [P, NT])
        alpha = sb("alpha", [P, NT])
        half_alpha = sb("half_alpha", [P, NT])
        is_best = sb("is_best", [P, NT, E])
        ranked = sb("ranked", [P, NT, E])
        best_rank = sb("best_rank", [P, NT])
        onehot = sb("onehot", [P, E, NT])
        over = sb("over", [P, E, NT])
        tiles_e = sb("tiles_e", [P, 1 + E])
        tiles_upto = sb("tiles_upto", [P, 1 + E])
        run = sb("run", [P, E, NT])
        rank_at = sb("rank_at", [P, E, NT])
        placed_at = sb("placed_at", [P, E, NT])
        chosen_at = sb("chosen_at", [P, E, NT])
        pos = sb("pos", [P, NT], I32)
        tile_place = sb("tile_place", [P, 2, NT], I32)
        source = sb("source", [P, NS + 1], I32)
        taken_row = sb("taken_row", [P, NS + 1])
        empty_row = sb("empty_row", [P, NS + 1])
        target = sb("target", [P, NS + 1], I32)
        passed = sb("passed", [P, NS + 1, E])
        owner_f = sb("owner_f", [P, NS + 1])
        owner = sb("owner", [P, NS + 1], I32)

        rows_in = sb("rows_in", [P, 4, D])
        rec = sb("rec", [P, 4, REC])
        lnT = sb("lnT", [P, 2, P])
        hid = sb("hid", [P, 2, FC, P])
        rows_out = sb("rows_out", [P, 4, D])

        xa = sb("xa", [P, NB, D])
        xaT = sb("xaT", [P, NB, P])
        qT = sb("qT", [P, PAIRS, NB * P])
        kT = sb("kT", [P, PAIRS, NB * P])
        proj_wide = kT[:, :, :].rearrange("p r t -> p (r t)")[:, 0:H * M].rearrange("p (h m) -> p h m", m=M)
        f_turned = qT[:, :, :].rearrange("p r t -> p (r t)")[:, 0:NT * P].rearrange("p (t q) -> p t q", q=P)
        v_raw = sb("v_raw", [P, NB, D])
        v_pair = sb("v_pair", [P, GROUPS, NB, PAIRS, 32])
        v_head = sb("v_head", [P, GROUPS, NB, PAIRS, 2, 32])
        k_rows = sb("k_rows", [P, PAIRS, P])
        scores = sb("scores", [P, 2, 4, NB, P])
        hot = scores[:, :, :, :, :].rearrange("p a b c d -> p (a b c d)").bitcast(BF16)
        place_hot = hot[:, 0:NT * P].rearrange("p (t k) -> p t k", k=P)
        tile_hot = hot[:, NT * P:NT * (P + 3 * (NS + 1))].rearrange("p (t a s) -> p t a s", a=3, s=NS + 1)
        o_sb = sb("o_sb", [P, 2, P])
        den = sb("den", [P, PAIRS, 2])
        inv_den = sb("inv_den", [P, PAIRS, 2])
        heads_out = sb("heads_out", [P, PAIRS, 2, HD])
        heads_T = sb("heads_T", [P, P])
        proj_out = sb("proj_out", [P, D])
        stateT = sb("stateT", [P, 2, P])
        state = sb("state", [P, PAIRS, 32])

        x_loaded = [sem(f"x_loaded{q}") for q in range(NT // NB)]
        small_loaded = sem("small_loaded")
        attn_loaded = sem("attn_loaded")
        experts_loaded = sem("experts_loaded")
        filled = sem("filled")
        consts = sem("consts")
        cols_psum = sem("cols_psum")
        cols_ready = sem("cols_ready")
        records_ready = sem("records_ready")
        wide_ready = sem("wide_ready")
        w_turned_psum = sem("w_turned_psum")
        w_turned_sb = sem("w_turned_sb")
        w_feat_psum = sem("w_feat_psum")
        w_feat_sb = sem("w_feat_sb")
        b_feat_psum = sem("b_feat_psum")
        out_stored = sem("out_stored")
        ffn = [FfnSignals(sem, n) for n in range(2)]
        a_stats, a_aggr, a_dev, a_rstd, a_norm = (sem(f"a_{s}") for s in ("stats", "aggr", "dev", "rstd", "norm"))
        wide_done = sem("wide_done")
        wide_read = sem("wide_read")
        v_ready = sem("v_ready")
        scored = sem("scored")
        masked = sem("masked")
        o_done = sem("o_done")
        o_read = sem("o_read")
        o_turned = sem("o_turned")
        den_ready = sem("den_ready")
        inv_ready = sem("inv_ready")
        heads_ready = sem("heads_ready")
        heads_turned = sem("heads_turned")
        heads_T_ready = sem("heads_T_ready")
        projected = sem("projected")
        projected_sb = sem("projected_sb")
        residual = sem("residual")
        stateT_done = sem("stateT_done")
        stateT_added = sem("stateT_added")
        state_turned = sem("state_turned")
        state_ready = sem("state_ready")

        block = ctx.enter_context(nc.Block())

        def ring(o):
            return (1 + o) % 4

        def ring_value(i, o):
            return i * 4 + (12 + 16 * ((o + 1) // 4))

        def early(i, o, n):
            return isinstance(i, int) and i + o < n

        LOOP_FROM, LOOP_TO = 5, NS - 2

        WIDE_G = 2 + 2 * PAIRS + 2 * NB
        WIDE_B = GROUPS * WIDE_G - 2
        KEY_ROWS = 1 + 2 * PAIRS

        def wide(b, g, idx):
            return b * WIDE_B + (1 + WIDE_G * g + idx)

        def turn_idx(g):
            return WIDE_G - 1 if g < GROUPS - 1 else WIDE_G - 3

        @block.sync
        def _(sp):
            for q in range(NT // NB):
                sp.dma_start(x[:, q * NB:(q + 1) * NB, :],
                             x_in.rearrange("b (t p) d -> p (b t) d", p=P)[:, q * NB:(q + 1) * NB, :]
                             ).then_inc(x_loaded[q], 16)
            sp.wait_ge(small_loaded, 80)
            sp.dma_start(records[:, :, W1:W1 + F], w1.rearrange("e d f -> d e f")).then_inc(experts_loaded, 16)
            sp.dma_start(qkv_sb[:, :], qkv_w).then_inc(attn_loaded, 16)
            sp.dma_start(proj_sb[:, :], proj.rearrange("h d m -> (h d) m")).then_inc(attn_loaded, 16)
            for c in range(FC):
                sp.dma_start(records[:, :, W2 + c * D:W2 + (c + 1) * D],
                              w2[:, c * P:(c + 1) * P, :].rearrange("e p d -> p e d")).then_inc(experts_loaded, 16)
            sp.dma_start(records[:, :, B2:B2 + D],
                          b2.rearrange("(o e) d -> o e d", o=1).broadcast_to([P, E, D])).then_inc(experts_loaded, 16)
            sp.dma_start(v_bias[:, :], qkv_b.rearrange("(a d) -> a d", d=D)[2:3, :].broadcast_to([P, D])
                          ).then_inc(attn_loaded, 16)
            sp.dma_start(outw_sb[:, :], out_w).then_inc(attn_loaded, 16)
            sp.dma_start(out_bias[:, :], out_b.rearrange("(a d) -> a d", a=1).broadcast_to([P, D])
                          ).then_inc(attn_loaded, 16)
            for n in range(2):
                s = ffn[n]
                for q in range(NT // NB):
                    sp.wait_ge(s.norm2, NB * (q + 1))
                    sp.dma_start(xn_rows.rearrange("(t p) d -> p t d", p=P)[:, q * NB:(q + 1) * NB, :],
                                 xn[:, q * NB:(q + 1) * NB, :]).then_inc(s.xn_stored, 16)
                for o in range(-2, 2):
                    sp.wait_ge(s.rows_stored[ring(o)], ring_value(LOOP_TO, o))
                for q in range(NT // NB):
                    sp.dma_start(mix[:, q * NB:(q + 1) * NB, :],
                                 ffn_rows.rearrange("(t p) d -> p t d", p=P)[:, q * NB:(q + 1) * NB, :]
                                 ).then_inc(s.mix_loaded[q], 16)
                if n == 1:
                    for q in range(NT // NB):
                        sp.wait_ge(s.result, NB * (q + 1))
                        sp.dma_start(out.rearrange("b (t p) d -> p (b t) d", p=P)[:, q * NB:(q + 1) * NB, :],
                                     x[:, q * NB:(q + 1) * NB, :]).then_inc(out_stored, 16)
                    sp.wait_ge(out_stored, 16 * (NT // NB))

        @block.gpsimd
        def _(pool):
            fills = [(ident, 0.0), (later, -1.0), (causal, 1.0), (ones, 1.0), (head_block, 1.0)]
            for n, (t, value) in enumerate(fills):
                nc.gpsimd.memset(t[:, :], value).then_inc(filled, 1)
            nc.gpsimd.memset(eps_col[:, :], LN_EPS).then_inc(filled, 1)
            nc.gpsimd.memset(go_on[:, :, :], 1.0).then_inc(filled, 1)
            nc.gpsimd.memset(tiles_e[:, 0:1], 0.0).then_inc(filled, 1)
            pool.wait_ge(filled, 8)
            nc.gpsimd.memset(go_on[:, :, 0:1], 0.0).then_inc(filled, 1)
            nc.gpsimd.affine_select(out=ident[:, :], in_=ident[:, :], compare_op=ALU.not_equal, fill=1.0, base=0,
                                    pattern=[[-1, P]], channel_multiplier=1).then_inc(consts, 1)
            nc.gpsimd.affine_select(out=later[:, :], in_=later[:, :], compare_op=ALU.is_ge, fill=0.0, base=0,
                                    pattern=[[-1, P]], channel_multiplier=1).then_inc(consts, 1)
            nc.gpsimd.affine_select(out=causal[:, :], in_=causal[:, :], compare_op=ALU.is_ge, fill=0.0, base=0,
                                    pattern=[[1, P]], channel_multiplier=-1).then_inc(consts, 1)
            nc.gpsimd.iota(first_rank[:, :], pattern=[[-1, E]], base=E, channel_multiplier=0,
                           allow_small_or_imprecise_dtypes=True).then_inc(consts, 1)
            nc.gpsimd.iota(tile_edges[:, :], pattern=[[P, NT]], base=0, channel_multiplier=0,
                           allow_small_or_imprecise_dtypes=True).then_inc(consts, 1)
            nc.gpsimd.iota(slots[:, :], pattern=[[1, NS + 1]], base=0, channel_multiplier=0,
                           allow_small_or_imprecise_dtypes=True).then_inc(consts, 1)
            nc.gpsimd.iota(places[:, :], pattern=[[1, P]], base=0, channel_multiplier=0,
                           allow_small_or_imprecise_dtypes=True).then_inc(consts, 1)
            nc.gpsimd.iota(partition[:, :], pattern=[[0, 1]], base=0, channel_multiplier=1,
                           allow_small_or_imprecise_dtypes=True).then_inc(consts, 1)
            nc.gpsimd.iota(spare_row[:, :], pattern=[[P, NS + 1]], base=NT * P, channel_multiplier=1,
                           allow_small_or_imprecise_dtypes=True).then_inc(consts, 1)
            nc.gpsimd.affine_select(out=head_block[:, :], in_=head_block[:, :], compare_op=ALU.is_ge, fill=0.0,
                                    base=0, pattern=[[-HD, H]], channel_multiplier=1).then_inc(consts, 1)
            pool.wait_ge(consts, 10)
            nc.gpsimd.affine_select(out=head_block[:, :], in_=head_block[:, :], compare_op=ALU.is_ge, fill=0.0,
                                    base=HD - 1, pattern=[[HD, H]], channel_multiplier=-1).then_inc(consts, 1)
            nc.gpsimd.memset(x_all[:, 0:NB, :], 0.0).then_inc(filled, 1)
            nc.gpsimd.memset(x_all[:, NB + NT:NB + NT + NB, :], 0.0).then_inc(filled, 1)
            nc.gpsimd.memset(v_pair[:, :, :, :, :], 0.0).then_inc(filled, 1)
            nc.gpsimd.memset(v_head[:, :, :, :, :, :], 0.0).then_inc(filled, 1)
            pool.wait_ge(filled, 13)
            for g in range(GROUPS):
                for a in range(2):
                    nc.gpsimd.memset(v_pair[:, g, :, :, 9 * a + HD:9 * a + HD + 1], 1.0).then_inc(filled, 1)
                    nc.gpsimd.memset(v_head[:, g, :, :, a, 9 * a + HD:9 * a + HD + 1], 1.0).then_inc(filled, 1)
            pool.wait_ge(cols_ready, 1)
            nc.gpsimd.tensor_copy(records[:, :, B1:B1 + FC],
                                  cols[:, R_B1:R_B1 + E * FC].rearrange("p (e c) -> p e c", c=FC)
                                  ).then_inc(records_ready, 1)
            nc.gpsimd.tensor_copy(records[:, :, GG:GG + 1],
                                  cols[:, R_G:R_G + E].rearrange("p (e c) -> p e c", c=1)).then_inc(records_ready, 1)
            nc.gpsimd.tensor_copy(records[:, :, BB:BB + 1],
                                  cols[:, R_B:R_B + E].rearrange("p (e c) -> p e c", c=1)).then_inc(records_ready, 1)

            for n in range(2):
                s = ffn[n]
                if n == 1:
                    with pool.Fori(0, B) as b:
                        for g in range(GROUPS):
                            pool.wait_ge(wide_read, b * WIDE_B + (2 + WIDE_G * g))
                            src = v_raw[:, :, :].rearrange("p k (r a d) -> p k r a d", a=2, d=HD)
                            bias = v_bias[:, :].rearrange("p (r a d) -> p r a d", a=2, d=HD)
                            for k in range(NB):
                                nc.gpsimd.tensor_tensor(
                                    v_pair[:, g, k, :, 0:18].rearrange("p r (a d) -> p r a d", a=2)[:, :, :, 0:HD],
                                    src[:, k], bias, ALU.add).then_inc(v_ready, 1)
                                flat = v_head[:, g, k, :, :, :].rearrange("p r a w -> p r (a w)")
                                for a in range(2):
                                    nc.gpsimd.tensor_tensor(flat[:, :, 41 * a:41 * a + HD], src[:, k, :, a, :],
                                                            bias[:, :, a, :], ALU.add).then_inc(v_ready, 1)

                pool.wait_ge(s.xn_stored, 16 * (NT // NB))
                pool.wait_ge(s.sources, 1)
                AHEAD = 4
                for j in range(-AHEAD, NS):
                    m = j + AHEAD
                    if m < NS:
                        if m >= 4:
                            pool.wait_ge(s.rows_turned, m - 3)
                        pool.indirect_dma_start(
                            out=rows_in[:, m % 4, :], out_offset=None, in_=xn_rows[:, :],
                            in_offset=bass.IndirectOffsetOnAxis(ap=source[:, m:m + 1], axis=0)
                            ).then_inc(s.rows_loaded[m % 4], 16)
                    if j == 0:
                        pool.wait_ge(s.targets, 1)
                    if j >= 0:
                        pool.wait_ge(s.rows_out, j + 1)
                        pool.indirect_dma_start(
                            out=ffn_rows[:, :], out_offset=bass.IndirectOffsetOnAxis(ap=target[:, j:j + 1], axis=0),
                            in_=rows_out[:, j % 4, :], in_offset=None).then_inc(s.rows_stored[j % 4], 16)

        @block.scalar
        def _(act):
            act.dma_start(rows[R_B1:R_B1 + E * FC, :], b1.rearrange("e (c p) -> (e c) p", p=P)
                          ).then_inc(small_loaded, 16)
            act.dma_start(rows[R_G:R_G + E, :], ln_g).then_inc(small_loaded, 16)
            act.dma_start(rows[R_B:R_B + E, :], ln_b).then_inc(small_loaded, 16)
            act.dma_start(rows[R_C:R_C + E, :], centroids).then_inc(small_loaded, 16)
            act.dma_start(rows[R_QB:R_QB + 2, :], qkv_b.rearrange("(a d) -> a d", d=D)[0:2, :]
                          ).then_inc(small_loaded, 16)
            def deviation(out_ap, var_ap, signal):
                nc.scalar.activation(out_ap, var_ap, ACT.Sqrt, bias=eps_col[:, 0:1]).then_inc(signal, 1)

            def blocks(q):
                return slice(q * NB, (q + 1) * NB)

            act.wait_ge(filled, 6)
            nc.scalar.activation(warm[:, :], eps_col[:, :], ACT.Sqrt)
            for n in range(2):
                s = ffn[n]
                for step in range(NT // NB + 1):
                    if n == 0 and step < NT // NB:
                        act.wait_ge(s.aggr1, AGGR * (step + 1))
                        deviation(dev[:, blocks(step)], mv1[:, 1, blocks(step)], s.dev1)
                    if n == 1 and step == NT // NB - 1:
                        act.wait_ge(s.aggr1, AGGR * (NT // NB + 1))
                        deviation(dev_f[:, :], mv_f[:, 1, :], s.dev1)
                    q = step - 1
                    if q >= 0:
                        act.wait_ge(s.f_turned, q + 1)
                        nc.scalar.activation(f_turned[:, blocks(q), :], psum[:, q % 2, :], ACT.Copy
                                             ).then_inc(s.f_turned_sb, 1)
                act.wait_ge(s.var2, 2 if n == 0 else 2 * (NT // NB + 1))
                deviation(dev_b[:, :], var_b[:, NB:NB + NT], s.dev2)
                act.wait_ge(s.rstd2, 1)
                for t in range(NT):
                    nc.scalar.activation(xn[:, t, :], f[:, t, :], ACT.Copy, scale=rstd_b[:, t:t + 1]
                                         ).then_inc(s.norm2, 1)
                act.wait_ge(s.route, 1)
                nc.scalar.activation(alpha[:, :], best[:, :], ACT.Sigmoid).then_inc(s.gate, 1)

                def relu(i, o, par):
                    act.wait_ge(s.up, 2 * (i + o) + 1)
                    for c in range(FC // 2):
                        nc.scalar.activation(hid[:, par, c, :], psum[:, 4 + 2 * par, c * P:(c + 1) * P], ACT.Relu,
                                             bias=rec[:, ring(o), B1 + c:B1 + c + 1]).then_inc(s.relu_act, 1)

                def fetch(i, o):
                    at = act.value_load(owner[0:1, bass.ds(i + o, 1)], min_val=0, max_val=(E - 1) * REC)
                    if not early(i, o, 4):
                        act.wait_ge(s.rows_out, i + (o - 3))
                    flat = records[:, :, :].rearrange("p e r -> p (e r)")
                    nc.scalar.activation(rec[:, ring(o), :], flat[:, bass.ds(at, REC)], ACT.Copy
                                         ).then_inc(s.weights, 1)

                if n == 0:
                    act.wait_ge(experts_loaded, 16 * (2 + FC))
                    act.wait_ge(records_ready, 3)
                act.wait_ge(s.table, 1)
                for o in range(-1, 1):
                    fetch(1, o)
                for o in range(-1, 4):
                    fetch(1, o + 2)
                    relu(1, o, (1 + o) % 2)
                with act.Fori(LOOP_FROM, LOOP_TO - 3, 4) as i:
                    for o in range(4):
                        fetch(i, o + 2)
                        relu(i, o, (1 + o) % 2)
                for o in range(2):
                    relu(LOOP_TO, o, (1 + o) % 2)

                if n == 1:
                    continue
                act.wait_ge(w_turned_psum, 1)
                nc.scalar.activation(w_turned[:, :, :], psum[:, 4, 0:2 * P], ACT.Copy).then_inc(w_turned_sb, 1)
                for j in range(4):
                    act.wait_ge(w_feat_psum, j + 1)
                    nc.scalar.activation(w_feat[:, j // 2, (j % 2) * 512:(j % 2 + 1) * 512],
                                         psum[:, 4 + j, :], ACT.Copy).then_inc(w_feat_sb, 1)
                act.wait_ge(b_feat_psum, 1)
                nc.scalar.activation(b_feat[:, :, :], psum[:, 1, 0:2 * PAIRS], ACT.Copy).then_inc(w_feat_sb, 1)
                act.wait_ge(a_aggr, AGGR)
                deviation(dev_a[:, :], mv_a[:, 1, :], a_dev)
                act.wait_ge(wide_done, 1)
                nc.scalar.activation(xaT[:, :, :], psum[:, 0, :], ACT.Copy).then_inc(wide_read, 1)

                def keys_rows(b, g, k):
                    if (g, k) != (0, 0):
                        act.wait_ge(stateT_done, b * (CHUNKS - 1) + (NB * g + k))
                    for h in range(2):
                        idx = KEY_ROWS + 2 * k + h
                        act.wait_ge(wide_done, wide(b, g, idx) + 1)
                        nc.scalar.activation(k_rows[:, 4 * h:4 * h + 4, :], psum[:, (1 + idx) % 2, :], ACT.Copy
                                             ).then_inc(wide_read, 1)

                def heads_turn(b, c):
                    act.wait_ge(heads_turned, b * CHUNKS + (c + 1))
                    nc.scalar.activation(heads_T[:, :], psum[:, 6, 0:P], ACT.Copy).then_inc(heads_T_ready, 1)

                act.wait_ge(w_feat_sb, 5)
                with act.Fori(0, B) as b:
                    for g in range(GROUPS):
                        act.wait_ge(wide_done, wide(b, g, 0) + 1)
                        nc.scalar.activation(v_raw[:, :, :], psum[:, 1, :], ACT.Copy).then_inc(wide_read, 1)
                        for r in range(PAIRS):
                            for a, dst in ((0, qT), (1, kT)):
                                idx = 1 + 2 * r + a
                                act.wait_ge(wide_done, wide(b, g, idx) + 1)
                                nc.scalar.activation(dst[:, r, :], psum[:, (1 + idx) % 2, :], ACT.Relu,
                                                     bias=b_feat[:, r, a:a + 1]).then_inc(wide_read, 1)
                                if g == 1 and idx == 6:
                                    heads_turn(b, NB * g - 1)
                        act.wait_ge(ffn[1].aggr1, b * (AGGR * GROUPS) + AGGR * (g + 1))
                        deviation(dev_f[:, :], mv_f[:, 1, :], ffn[1].dev1)
                        for k in range(NB):
                            c = NB * g + k
                            if c < CHUNKS - 1:
                                keys_rows(b, g, k)
                            if k == NB - 1:
                                idx = turn_idx(g)
                                act.wait_ge(wide_done, wide(b, g, idx) + 1)
                                nc.scalar.activation(xaT[:, :, :], psum[:, (1 + idx) % 2, :], ACT.Copy
                                                     ).then_inc(wide_read, 1)
                            act.wait_ge(o_done, b * CHUNKS + (c + 1))
                            nc.scalar.activation(o_sb[:, :, :], psum[:, 6, 0:2 * P], ACT.Copy).then_inc(o_read, 1)
                            if k == 1:
                                act.wait_ge(a_aggr, b * (AGGR * GROUPS) + AGGR * (g + 2))
                                deviation(dev_a[:, :], mv_a[:, 1, :], a_dev)
                            if k < NB - 1 or g == GROUPS - 1:
                                heads_turn(b, c)

        @block.tensor
        def _(pe):
            def turn(bank, at, src):
                return nc.tensor.transpose(psum[:, bank, at:at + src.shape[0]], src, ident[0:src.shape[0], 0:src.shape[0]])

            pe.wait_ge(consts, 1)
            pe.wait_ge(small_loaded, 80)
            nc.tensor.transpose(psum[:, 3, 0:NR], rows[:, :], ident[0:NR, 0:NR]).then_inc(cols_psum, 1)

            for n in range(2):
                s = ffn[n]
                for q in range(NT // NB + 1):
                    if q < NT // NB:
                        pe.wait_ge(s.norm1, NB * (q + 1 + n))
                        if q >= 2:
                            pe.wait_ge(s.f_turned_sb, q - 1)
                        for t in range(NB):
                            last = turn(q % 2, t * P, f[:, q * NB + t, :])
                        last.then_inc(s.f_turned, 1)
                    if q > 0:
                        pe.wait_ge(s.f_turned_sb, q)
                        if n == 0 and q == 1:
                            pe.wait_ge(cols_ready, 1)
                        for t in range((q - 1) * NB, q * NB):
                            last = nc.tensor.matmul(psum[:, 2, t * E:(t + 1) * E], f_turned[:, t, :],
                                                    cols[:, R_C:R_C + E], start=True, stop=True)
                last.then_inc(s.affinity, 1)
                if n == 0:
                    pe.wait_ge(consts, 11)
                pe.wait_ge(s.onehot, 1)
                hot = onehot[:, :, :].rearrange("p e t -> p (e t)")
                nc.tensor.matmul(psum[:, 3, 0:E * NT], later[:, :], hot, start=True, stop=True)
                nc.tensor.matmul(psum[:, 3, E * NT:2 * E * NT], ones[:, :], hot, start=True, stop=True
                                 ).then_inc(s.counts, 1)

                for q in range(NT // NB):
                    pe.wait_ge(s.place_hot, q + 1)
                    for t in range(q * NB, (q + 1) * NB):
                        last = nc.tensor.matmul(psum[:, 2, 0:3 * (NS + 1)], place_hot[:, t, :],
                                                tile_hot[:, t, :, :].rearrange("p a s -> p (a s)"),
                                                start=(t == 0), stop=(t == NT - 1))
                last.then_inc(s.inverse, 1)
                def turn_rows(i, o, par):
                    pe.wait_ge(s.rows_loaded[ring(o)], ring_value(i, o))
                    turn(par, 0, rows_in[:, ring(o), :]).then_inc(s.rows_turned, 1)

                def up(i, o, par):
                    pe.wait_ge(s.inputs, i + (o + 1))
                    for c in range(FC):
                        last = nc.tensor.matmul(psum[:, 4 + 2 * par + c // 2, (c % 2) * P:(c % 2 + 1) * P],
                                                rec[:, ring(o), W1 + c * P:W1 + (c + 1) * P], lnT[:, par, :],
                                                start=True, stop=True)
                        if c % 2:
                            last.then_inc(s.up, 1)

                def down(i, o, par):
                    pe.wait_ge(s.relu_act, 2 * (i + o) + 2)
                    pe.wait_ge(s.relu_dve, 2 * (i + o) + 2)
                    for c in range(FC):
                        last = nc.tensor.matmul(psum[:, 2 + par, 0:D], hid[:, par, c, :],
                                                rec[:, ring(o), W2 + c * D:W2 + (c + 1) * D],
                                                start=(c == 0), stop=(c == FC - 1))
                    last.then_inc(s.down, 1)

                def tile_step(i, o):
                    up(i, o, (1 + o) % 2)
                    if not (isinstance(i, int) and i + o == NS - 1):
                        turn_rows(i, o + 1, o % 2)
                    if not early(i, o, 1):
                        down(i, o - 1, o % 2)

                pe.wait_ge(s.targets, 1)
                turn_rows(1, -1, 0)
                for o in range(-1, 4):
                    tile_step(1, o)
                with pe.Fori(LOOP_FROM, LOOP_TO - 3, 4) as i:
                    for o in range(4):
                        tile_step(i, o)
                for o in range(2):
                    tile_step(LOOP_TO, o)
                down(LOOP_TO, 1, 0)

                if n == 1:
                    continue
                pe.wait_ge(attn_loaded, 80)
                for a in range(2):
                    last = turn(4, a * P, qkv_sb[:, a * D:(a + 1) * D])
                last.then_inc(w_turned_psum, 1)
                pe.wait_ge(w_turned_sb, 1)
                pe.wait_ge(wide_ready, 1)
                wide_flat = proj_wide[:, :, :].rearrange("p h m -> p (h m)")
                for j in range(4):
                    nc.tensor.matmul(psum[:, 4 + j, :], w_turned[:, j // 2, :],
                                     wide_flat[:, (j % 2) * 512:(j % 2 + 1) * 512], start=True, stop=True
                                     ).then_inc(w_feat_psum, 1)
                for r in range(PAIRS):
                    last = nc.tensor.matmul(psum[:, 1, 2 * r:2 * r + 2], wide_flat[:, r * P:(r + 1) * P],
                                            cols[:, R_QB:R_QB + 2], start=True, stop=True)
                last.then_inc(b_feat_psum, 1)
                pe.wait_ge(a_norm, NB)
                for t in range(NB):
                    last = turn(0, t * P, xa[:, t, :])
                last.then_inc(wide_done, 1)

                def values(b, g):
                    pe.wait_ge(wide_read, wide(b, g, 0))
                    for k in range(NB):
                        last = nc.tensor.matmul(psum[:, 1, k * P:(k + 1) * P], xaT[:, k, :], qkv_sb[:, 2 * D:3 * D],
                                                start=True, stop=True)
                    last.then_inc(wide_done, 1)

                def features(b, g, r):
                    for a in range(2):
                        idx = 1 + 2 * r + a
                        pe.wait_ge(wide_read, wide(b, g, idx) - 1)
                        nc.tensor.matmul(psum[:, (1 + idx) % 2, :], w_feat[:, a, r * P:(r + 1) * P],
                                         xaT[:, :, :].rearrange("p k t -> p (k t)"), start=True, stop=True
                                         ).then_inc(wide_done, 1)

                def score(g, k, half):
                    at = slice(k * P, (k + 1) * P)
                    for r in range(4):
                        for a in range(2):
                            last = nc.tensor.matmul(psum[:, 2 + 2 * half + a, r * P:(r + 1) * P],
                                                    kT[64 * a:64 * a + 64, 4 * half + r, at],
                                                    qT[64 * a:64 * a + 64, 4 * half + r, at], start=True, stop=True)
                            if r == 3:
                                last.then_inc(scored, 1)

                def key_rows(b, g, k):
                    for h in range(2):
                        idx = KEY_ROWS + 2 * k + h
                        pe.wait_ge(wide_read, wide(b, g, idx) - 1)
                        for r in range(4):
                            last = turn((1 + idx) % 2, r * P, kT[:, 4 * h + r, k * P:(k + 1) * P])
                        last.then_inc(wide_done, 1)

                def turn_next(b, g):
                    idx = turn_idx(g)
                    pe.wait_ge(wide_read, wide(b, g, idx) - 1)
                    pe.wait_ge(a_norm, b * (NB * GROUPS) + NB * (g + 2))
                    for t in range(NB):
                        last = turn((1 + idx) % 2, t * P, xa[:, t, :])
                    last.then_inc(wide_done, 1)

                def context(b, g, k):
                    c = NB * g + k
                    pe.wait_ge(state_ready, b * CHUNKS + (c + 1))
                    if c > 0:
                        pe.wait_ge(projected_sb, b * CHUNKS + c)
                    for half in range(2):
                        for r in range(4):
                            nc.tensor.matmul(psum[32 * r:32 * r + 32, 6, half * P:(half + 1) * P],
                                             state[:, 4 * half + r, :], qT[:, 4 * half + r, k * P:(k + 1) * P],
                                             start=(half == 0), stop=False, skip_group_check=True)
                    if k == 0:
                        pe.wait_ge(v_ready, b * (3 * CHUNKS) + 3 * NB * (g + 1))
                    for half in range(2):
                        for a in range(2):
                            pe.wait_ge(masked, b * (4 * CHUNKS) + (4 * c + 2 * half + a + 1))
                            for r in range(4):
                                last = nc.tensor.matmul(psum[32 * r:32 * r + 32, 6, half * P:(half + 1) * P],
                                                        v_head[:, g, k, 4 * half + r, a, :],
                                                        scores[:, k % 2, 2 * half + a, r, :],
                                                        start=False, stop=(half == 1 and a == 1),
                                                        skip_group_check=True)
                    last.then_inc(o_done, 1)

                def turn_context(b, c):
                    pe.wait_ge(o_read, b * CHUNKS + (c + 1))
                    for half in range(2):
                        last = turn(6, half * P, o_sb[:, half, :])
                    last.then_inc(o_turned, 1)

                def state_sums(b, g, k):
                    pe.wait_ge(wide_read, wide(b, g, KEY_ROWS + 2 * k + 1) + 1)
                    for half in range(2):
                        for r in range(4):
                            last = nc.tensor.matmul(psum[32 * r:32 * r + 32, 7, half * P:(half + 1) * P],
                                                    v_pair[:, g, k, 4 * half + r, :], k_rows[:, 4 * half + r, :],
                                                    start=True, stop=True)
                    last.then_inc(stateT_done, 1)

                def turn_state(b, c):
                    pe.wait_ge(stateT_added, b * (CHUNKS - 1) + (c + 1))
                    for half in range(2):
                        last = turn(7, half * P, stateT[:, half, :])
                    last.then_inc(state_turned, 1)

                def turn_heads(b, c):
                    pe.wait_ge(heads_ready, b * CHUNKS + (c + 1))
                    turn(6, 0, heads_out[:, :, :, :].rearrange("p r a d -> p (r a d)")).then_inc(heads_turned, 1)

                def project(b, c):
                    pe.wait_ge(heads_T_ready, b * CHUNKS + (c + 1))
                    nc.tensor.matmul(psum[:, 6, 0:D], heads_T[:, :], outw_sb[:, :], start=True, stop=True
                                     ).then_inc(projected, 1)

                with pe.Fori(0, B) as b:
                    for g in range(GROUPS):
                        values(b, g)
                        for r in range(PAIRS):
                            features(b, g, r)
                            if g > 0:
                                if r == 0:
                                    turn_context(b, NB * g - 1)
                                    state_sums(b, g - 1, NB - 1)
                                if r == 1:
                                    turn_heads(b, NB * g - 1)
                                    turn_state(b, NB * g - 1)
                                if r == 4:
                                    project(b, NB * g - 1)
                        pe.wait_ge(wide_read, wide(b, g, 2 * PAIRS) + 1)
                        for half in range(2):
                            score(g, 0, half)
                        for k in range(NB):
                            c = NB * g + k
                            if c < CHUNKS - 1:
                                key_rows(b, g, k)
                            if k == NB - 1:
                                turn_next(b, g)
                            context(b, g, k)
                            if k < NB - 1:
                                score(g, k + 1, 0)
                                turn_context(b, c)
                                state_sums(b, g, k)
                                score(g, k + 1, 1)
                                turn_heads(b, c)
                                turn_state(b, c)
                                project(b, c)
                            elif g == GROUPS - 1:
                                turn_context(b, c)
                                turn_heads(b, c)
                                project(b, c)

        @block.vector
        def _(dve):
            def norm_stats(source, stats_to, mv, stats_signal, aggr_signal, blocks_before):
                for k in range(NB):
                    nc.vector.bn_stats(stats_to[:, k, :], source(k)).then_inc(stats_signal, 1)
                steps = blocks_before * AGGR
                dve.wait_ge(stats_signal, (blocks_before + 1) * NB)
                nc.vector.tensor_tensor(halves[:, 0, :], stats_to[:, :, 1], stats_to[:, :, 4], ALU.add
                                        ).then_inc(aggr_signal, 1)
                nc.vector.tensor_tensor(halves[:, 1, :], stats_to[:, :, 1], stats_to[:, :, 4], ALU.subtract
                                        ).then_inc(aggr_signal, 1)
                nc.vector.tensor_tensor(halves[:, 2, :], stats_to[:, :, 2], stats_to[:, :, 5], ALU.add
                                        ).then_inc(aggr_signal, 1)
                dve.wait_ge(aggr_signal, steps + 3)
                nc.vector.scalar_tensor_tensor(out=halves[:, 3, :], in0=halves[:, 1, :], scalar=0.25,
                                               in1=halves[:, 1, :], op0=ALU.mult, op1=ALU.mult
                                               ).then_inc(aggr_signal, 1)
                nc.vector.tensor_scalar(mv[:, 0, :], halves[:, 0, :], 0.5, None, ALU.mult).then_inc(aggr_signal, 1)
                dve.wait_ge(aggr_signal, steps + 5)
                nc.vector.scalar_tensor_tensor(out=mv[:, 1, :], in0=halves[:, 2, :], scalar=1.0 / D,
                                               in1=halves[:, 3, :], op0=ALU.mult, op1=ALU.add
                                               ).then_inc(aggr_signal, 1)

            def norm_apply(source, dest, mv, dev_, rstd_, dev_signal, rstd_signal, norm_signal, blocks_before):
                dve.wait_ge(dev_signal, blocks_before + 1)
                nc.vector.reciprocal(rstd_, dev_).then_inc(rstd_signal, 1)
                dve.wait_ge(rstd_signal, blocks_before + 1)
                for k in range(NB):
                    nc.vector.tensor_scalar(dest(k), source(k), mv[:, 0, k:k + 1], rstd_[:, k:k + 1],
                                            ALU.subtract, ALU.mult).then_inc(norm_signal, 1)

            def tiles_of(data, first):
                return lambda k: data[:, bass.ds(first + k, 1), :].squeeze(1)

            def variance_of_normed(to, shrunk_, var, rstd_, signal, blocks_before):
                nc.vector.tensor_tensor(shrunk_, var, rstd_, ALU.mult).then_inc(signal, 1)
                dve.wait_ge(signal, blocks_before * 2 + 1)
                nc.vector.tensor_tensor(to, shrunk_, rstd_, ALU.mult).then_inc(signal, 1)

            def second_stats(blocks_before):
                norm_stats(tiles_of(x_all, blocks_before * NB), stats_f, mv_f, ffn[1].stats1, ffn[1].aggr1,
                           blocks_before)

            def second_apply(blocks_before):
                norm_apply(tiles_of(x_all, blocks_before * NB), tiles_of(f_all, blocks_before * NB), mv_f,
                           dev_f[:, :], rstd_f[:, :], ffn[1].dev1, ffn[1].rstd1, ffn[1].norm1, blocks_before)
                variance_of_normed(var_b[:, bass.ds(blocks_before * NB, NB)], shrunk_f[:, :], mv_f[:, 1, :],
                                   rstd_f[:, :], ffn[1].var2, blocks_before)

            for n in range(2):
                s = ffn[n]
                if n == 0:
                    for step in range(NT // NB + 1):
                        if step < NT // NB:
                            q = slice(step * NB, (step + 1) * NB)
                            dve.wait_ge(x_loaded[step], 16)
                            norm_stats(tiles_of(x, step * NB), stats[:, q, :], mv1[:, :, q], s.stats1, s.aggr1, step)
                        if step == 1:
                            dve.wait_ge(cols_psum, 1)
                            nc.vector.tensor_copy(cols[:, :], psum[:, 3, 0:NR]).then_inc(cols_ready, 1)
                        if step > 0:
                            q = slice((step - 1) * NB, step * NB)
                            norm_apply(tiles_of(x, (step - 1) * NB), tiles_of(f, (step - 1) * NB), mv1[:, :, q],
                                       dev[:, q], rstd[:, q], s.dev1, s.rstd1, s.norm1, step - 1)
                    variance_of_normed(var_b[:, NB:NB + NT], shrunk[:, :], mv1[:, 1, :], rstd[:, :], s.var2, 0)
                else:
                    second_stats(NT // NB)
                    second_apply(NT // NB)

                route = [0]

                def link(ins, count=1):
                    route[0] += count
                    ins.then_inc(s.route, 1)
                    dve.wait_ge(s.route, route[0])

                def over_t(ap, width):
                    return ap.unsqueeze(2).broadcast_to([P, ap.shape[1], width])

                def over_first(ap, count):
                    return ap.unsqueeze(1).broadcast_to([P, count, ap.shape[1]])

                dve.wait_ge(s.dev2, 1)
                nc.vector.reciprocal(rstd_b[:, :], dev_b[:, :]).then_inc(s.rstd2, 1)
                dve.wait_ge(s.affinity, 1)
                if n == 0:
                    dve.wait_ge(consts, 11)
                aff = psum[:, 2, 0:NT * E].rearrange("p (t e) -> p t e", e=E)
                link(nc.vector.reduce_max(best[:, :], aff, AX_X))
                link(nc.vector.tensor_tensor(is_best[:, :, :], aff, over_t(best[:, :], E), ALU.is_ge))
                link(nc.vector.tensor_tensor(ranked[:, :, :], is_best[:, :, :], over_first(first_rank[:, :], NT), ALU.mult))
                link(nc.vector.reduce_max(best_rank[:, :], ranked[:, :, :], AX_X))
                nc.vector.tensor_tensor(onehot[:, :, :].rearrange("p e t -> p t e"), ranked[:, :, :],
                                        over_t(best_rank[:, :], E), ALU.is_equal).then_inc(s.onehot, 1)
                dve.wait_ge(s.counts, 1)
                dve.wait_ge(s.onehot, 1)
                if n == 0:
                    dve.wait_ge(filled, 9)
                flat = lambda ap: ap.rearrange("p e t -> p (e t)")
                link(nc.vector.tensor_tensor_scan(flat(run[:, :, :]), flat(go_on[:, :, :]),
                                                  psum[:, 3, E * NT:2 * E * NT], 0.0, ALU.mult, ALU.add))
                link(nc.vector.tensor_tensor(over[:, :, :], over_t(run[:, :, NT - 1], NT),
                                             over_first(tile_edges[:, :], E), ALU.is_gt))
                nc.vector.reduce_sum(tiles_e[:, 1:1 + E], over[:, :, :], AX_X).then_inc(s.route, 1)
                link(nc.vector.tensor_tensor(flat(rank_at[:, :, :]), psum[:, 3, 0:E * NT], flat(run[:, :, :]),
                                             ALU.add), 2)
                link(nc.vector.tensor_tensor_scan(tiles_upto[:, :], ones[:, 0:1 + E], tiles_e[:, :], 0.0,
                                                  ALU.mult, ALU.add))
                link(nc.vector.scalar_tensor_tensor(out=placed_at[:, :, :], in0=over_t(tiles_upto[:, 0:E], NT),
                                                    scalar=float(P), in1=rank_at[:, :, :],
                                                    op0=ALU.mult, op1=ALU.add))
                link(nc.vector.tensor_tensor(chosen_at[:, :, :], placed_at[:, :, :], onehot[:, :, :], ALU.mult))
                with nc.allow_low_precision("whole numbers below 4096"):
                    link(nc.vector.reduce_sum(pos[:, :], chosen_at[:, :, :].rearrange("p e t -> p t e"), AX_X))
                nc.vector.tensor_scalar(tile_place[:, 0, :], pos[:, :], P.bit_length() - 1, None,
                                        ALU.logical_shift_right).then_inc(s.route, 1)
                link(nc.vector.tensor_scalar(tile_place[:, 1, :], pos[:, :], P - 1, None, ALU.bitwise_and), 2)
                link(nc.vector.tensor_tensor(tile_hot[:, :, 0, :], over_t(tile_place[:, 0, :], NS + 1),
                                             over_first(slots[:, :], NT), ALU.is_equal))
                nc.vector.tensor_scalar(tile_hot[:, :, 1, :], tile_hot[:, :, 0, :], partition[:, 0:1], None,
                                        ALU.mult)
                nc.vector.tensor_tensor(tile_hot[:, :, 2, :], tile_hot[:, :, 0, :],
                                        over_t(tile_edges[:, :], NS + 1), ALU.mult)
                for q in range(NT // NB):
                    nc.vector.tensor_tensor(place_hot[:, q * NB:(q + 1) * NB, :], over_first(places[:, :], NB),
                                            over_t(tile_place[:, 1, q * NB:(q + 1) * NB], P), ALU.is_equal
                                            ).then_inc(s.place_hot, 1)
                if n == 0:
                    dve.wait_ge(attn_loaded, 80)
                    nc.vector.tensor_tensor(proj_wide[:, :, :], over_first(proj_sb[:, :], H),
                                            over_t(head_block[:, :], M), ALU.mult).then_inc(wide_ready, 1)
                dve.wait_ge(s.inverse, 1)
                inv = psum[:, 2, 0:3 * (NS + 1)].rearrange("p (a s) -> p a s", a=3)
                with nc.allow_low_precision("whole numbers below 4096"):
                    nc.vector.reduce_sum(source[:, :], inv[:, 1:3, :].rearrange("p a s -> p s a"), AX_X
                                         ).then_inc(s.sources, 1)
                link(nc.vector.tensor_tensor(passed[:, :, :], over_t(slots[:, :], E), over_first(tiles_upto[:, 1:1 + E], NS + 1), ALU.is_ge))
                link(nc.vector.reduce_sum(owner_f[:, :], passed[:, :, :], AX_X))
                nc.vector.tensor_scalar(owner[:, :], owner_f[:, :], float(E - 1), float(REC), ALU.min, ALU.mult
                                        ).then_inc(s.table, 1)
                link(nc.vector.tensor_tensor(taken_row[:, :], inv[:, 0, :], spare_row[:, :], ALU.mult))
                link(nc.vector.tensor_tensor(empty_row[:, :], spare_row[:, :], taken_row[:, :], ALU.subtract))
                dve.wait_ge(s.sources, 1)
                nc.vector.tensor_tensor(target[:, :], source[:, :], empty_row[:, :], ALU.add).then_inc(s.targets, 1)

                for q in range(NT // NB):
                    at = slice(q * NB, (q + 1) * NB)
                    nc.vector.scalar_tensor_tensor(out=x[:, at, :], in0=f[:, at, :], scalar=0.5, in1=x[:, at, :],
                                                   op0=ALU.mult, op1=ALU.add).then_inc(s.halved, 1)
                dve.wait_ge(s.gate, 1)
                nc.vector.tensor_scalar(half_alpha[:, :], alpha[:, :], 0.5, None, ALU.mult).then_inc(s.halved, 1)

                def scaled(i, o, par):
                    dve.wait_ge(s.rows_turned, i + (o + 1))
                    dve.wait_ge(s.weights, i + (o + 1))
                    nc.vector.tensor_scalar(lnT[:, par, :], psum[:, par, 0:P], rec[:, ring(o), GG:GG + 1],
                                            rec[:, ring(o), BB:BB + 1], ALU.mult, ALU.add).then_inc(s.inputs, 1)

                def relu(i, o, par):
                    dve.wait_ge(s.up, 2 * (i + o) + 2)
                    for c in range(FC // 2, FC):
                        nc.vector.tensor_scalar(hid[:, par, c, :], psum[:, 5 + 2 * par, (c - 2) * P:(c - 1) * P],
                                                rec[:, ring(o), B1 + c:B1 + c + 1], 0.0, ALU.add, ALU.max
                                                ).then_inc(s.relu_dve, 1)

                def result(i, o, par):
                    dve.wait_ge(s.down, i + (o + 1))
                    if not early(i, o, 4):
                        dve.wait_ge(s.rows_stored[ring(o)], ring_value(i, o - 4))
                    nc.vector.tensor_tensor(rows_out[:, ring(o), :], psum[:, 2 + par, 0:D],
                                            rec[:, ring(o), B2:B2 + D], ALU.add).then_inc(s.rows_out, 1)

                def tile_step(i, o):
                    if not (isinstance(i, int) and i + o == NS - 1):
                        scaled(i, o + 1, o % 2)
                    relu(i, o, (1 + o) % 2)
                    if not early(i, o, 1):
                        result(i, o - 1, o % 2)

                scaled(1, -1, 0)
                for o in range(-1, 4):
                    tile_step(1, o)
                with dve.Fori(LOOP_FROM, LOOP_TO - 3, 4) as i:
                    for o in range(4):
                        tile_step(i, o)
                for o in range(2):
                    tile_step(LOOP_TO, o)
                result(LOOP_TO, 1, 0)

                def add_ffn(q):
                    dve.wait_ge(s.mix_loaded[q], 16)
                    for t in range(q * NB, (q + 1) * NB):
                        nc.vector.scalar_tensor_tensor(out=x[:, t, :], in0=mix[:, t, :], scalar=half_alpha[:, t:t + 1],
                                                       in1=x[:, t, :], op0=ALU.mult, op1=ALU.add
                                                       ).then_inc(s.result, 1)

                dve.wait_ge(s.halved, NT // NB + 1)
                add_ffn(0)
                if n == 0:
                    dve.wait_ge(s.result, NB)
                    norm_stats(tiles_of(x, 0), stats_a, mv_a, a_stats, a_aggr, 0)
                    norm_apply(tiles_of(x, 0), tiles_of(xa, 0), mv_a, dev_a[:, :], rstd_a[:, :],
                               a_dev, a_rstd, a_norm, 0)
                for q in range(1, NT // NB):
                    add_ffn(q)
                if n == 1:
                    continue

                dve.wait_ge(s.result, NT)
                dve.wait_ge(filled, 13)
                dve.wait_ge(consts, 11)

                def mask(b, c, quad):
                    dve.wait_ge(scored, b * (4 * CHUNKS) + (4 * c + quad + 1))
                    nc.vector.tensor_tensor(scores[:, c % 2, quad, :, :],
                                            psum[:, 2 + quad, :].rearrange("p (r t) -> p r t", t=P),
                                            over_first(causal[:, :], NB), ALU.mult).then_inc(masked, 1)

                ctx4 = psum[:, 6, 0:2 * P].rearrange("p (r w) -> p r w", w=32)[:, :, 0:18].rearrange(
                    "p r (a w) -> p r a w", a=2)

                def divide(b, c):
                    dve.wait_ge(o_turned, b * CHUNKS + (c + 1))
                    nc.vector.tensor_scalar(den[:, :, :].unsqueeze(3), ctx4[:, :, :, HD:HD + 1], DEN_EPS, None,
                                            ALU.add).then_inc(den_ready, 1)
                    dve.wait_ge(den_ready, b * CHUNKS + (c + 1))
                    nc.vector.reciprocal(inv_den[:, :, :], den[:, :, :]).then_inc(inv_ready, 1)
                    dve.wait_ge(inv_ready, b * CHUNKS + (c + 1))
                    nc.vector.tensor_tensor(heads_out[:, :, :, :], ctx4[:, :, :, 0:HD],
                                            inv_den[:, :, :].unsqueeze(3).broadcast_to([P, PAIRS, 2, HD]),
                                            ALU.mult).then_inc(heads_ready, 1)

                def add_state(b, c):
                    dve.wait_ge(stateT_done, b * (CHUNKS - 1) + (c + 1))
                    sums = psum[:, 7, 0:2 * P].rearrange("p (h m) -> p h m", m=P)
                    if c == 0:
                        nc.vector.tensor_copy(stateT[:, :, :], sums).then_inc(stateT_added, 1)
                    else:
                        dve.wait_ge(stateT_added, b * (CHUNKS - 1) + c)
                        nc.vector.tensor_tensor(stateT[:, :, :], sums, stateT[:, :, :], ALU.add
                                                ).then_inc(stateT_added, 1)

                def split_state(b, c):
                    dve.wait_ge(state_turned, b * (CHUNKS - 1) + (c + 1))
                    dve.wait_ge(state_ready, b * CHUNKS + (c + 1))
                    turned = psum[:, 7, 0:2 * P].rearrange("p (r w) -> p r w", w=32)
                    nc.vector.tensor_copy(state[0:64, :, 0:9], turned[0:64, :, 0:9])
                    nc.vector.tensor_copy(state[64:P, :, 9:18], turned[64:P, :, 9:18]).then_inc(state_ready, 1)

                def add_out(b, c):
                    dve.wait_ge(projected, b * CHUNKS + (c + 1))
                    if c > 0:
                        dve.wait_ge(residual, b * CHUNKS + c)
                    nc.vector.tensor_tensor(proj_out[:, :], psum[:, 6, 0:D], out_bias[:, :], ALU.add
                                            ).then_inc(projected_sb, 1)
                    dve.wait_ge(projected_sb, b * CHUNKS + (c + 1))
                    at = bass.ds(b * CHUNKS + c, 1)
                    nc.vector.tensor_tensor(x[:, at, :], x[:, at, :], proj_out[:, :].unsqueeze(1), ALU.add
                                            ).then_inc(residual, 1)

                with dve.Fori(0, B) as b:
                    nc.vector.memset(state[:, :, :], 0.0).then_inc(state_ready, 1)
                    for g in range(GROUPS):
                        done = NB * g - 1
                        if g > 0:
                            divide(b, done)
                            add_state(b, done)
                            split_state(b, done)
                            add_out(b, done)
                            dve.wait_ge(residual, b * CHUNKS + NB * g)
                        second_stats(b * GROUPS + g)
                        second_apply(b * GROUPS + g)
                        for quad in range(4):
                            mask(b, NB * g, quad)
                        blocks = b * GROUPS + (g + 1)
                        for k in range(NB):
                            c = NB * g + k
                            next_x = tiles_of(x_all, (blocks + 1) * NB)
                            if k == 0:
                                norm_stats(next_x, stats_a, mv_a, a_stats, a_aggr, blocks)
                            if k == 1:
                                norm_apply(next_x, tiles_of(xa, 0), mv_a, dev_a[:, :], rstd_a[:, :],
                                           a_dev, a_rstd, a_norm, blocks)
                            if k < NB - 1:
                                mask(b, c + 1, 0)
                                mask(b, c + 1, 1)
                                divide(b, c)
                                add_state(b, c)
                                mask(b, c + 1, 2)
                                mask(b, c + 1, 3)
                                split_state(b, c)
                                add_out(b, c)
                            elif g == GROUPS - 1:
                                divide(b, c)
                                add_out(b, c)
                    dve.wait_ge(residual, b * CHUNKS + CHUNKS)


_ORDER = ["L0_attn_x", "L0_attn_qkv_w", "L0_attn_qkv_b", "L0_attn_out_w", "L0_attn_out_b", "L0_attn_proj",
          "L0_ffn_centroids", "L0_ffn_ln_g", "L0_ffn_ln_b", "L0_ffn_w1", "L0_ffn_b1", "L0_ffn_w2", "L0_ffn_b2"]


def kernel(**inputs):
    import numpy as _np
    import concourse.bacc as _bacc
    from concourse import mybir as _mybir
    from concourse.bass_utils import run_bass_kernel_spmd as _run

    nc = _bacc.Bacc("TRN2", target_bir_lowering=False, num_devices=1)
    arrays, args = {}, []
    for name in _ORDER:
        a = _np.ascontiguousarray(inputs[name])
        arrays[f"in_{name}"] = a
        args.append(nc.dram_tensor(f"in_{name}", a.shape, _mybir.dt.from_np(a.dtype), kind="ExternalInput").ap())
    shape = tuple(inputs["L0_attn_x"].shape)
    out = nc.dram_tensor("out_x", shape, F32, kind="ExternalOutput").ap()
    macaron_block(nc, *args, out)
    r = _run(nc, [arrays], core_ids=[0])
    return r.results[0]["out_x"]
```

```python
from contextlib import ExitStack

import concourse.bass as bass
from concourse import mybir

P = 128
F32 = mybir.dt.float32
I32 = mybir.dt.int32
F32R = mybir.dt.float32r
BF16 = mybir.dt.bfloat16
ALU = mybir.AluOpType
ACT = mybir.ActivationFunctionType
AX_X = mybir.AxisListType.X
LN_EPS = 1e-5
DEN_EPS = 1e-6


class FfnSignals:

    def __init__(self, sem, n):
        self.stats1 = sem(f"stats1_{n}")
        self.aggr1 = sem(f"aggr1_{n}")
        self.dev1 = sem(f"dev1_{n}")
        self.rstd1 = sem(f"rstd1_{n}")
        self.norm1 = sem(f"norm1_{n}")
        self.var2 = sem(f"var2_{n}")
        self.dev2 = sem(f"dev2_{n}")
        self.rstd2 = sem(f"rstd2_{n}")
        self.norm2 = sem(f"norm2_{n}")
        self.token_rows = sem(f"token_rows_{n}")
        self.f_turned = sem(f"f_turned_{n}")
        self.f_turned_sb = sem(f"f_turned_sb_{n}")
        self.affinity = sem(f"affinity_{n}")
        self.gate = sem(f"gate_{n}")
        self.route = sem(f"route_{n}")
        self.onehot = sem(f"onehot_{n}")
        self.counts = sem(f"counts_{n}")
        self.table = sem(f"table_{n}")
        self.place_hot = sem(f"place_hot_{n}")
        self.inverse = sem(f"inverse_{n}")
        self.sources = sem(f"sources_{n}")
        self.targets = sem(f"targets_{n}")
        self.weights = sem(f"weights_{n}")
        self.rows_turned = sem(f"rows_turned_{n}")
        self.inputs = sem(f"inputs_{n}")
        self.up = sem(f"up_{n}")
        self.relu_act = sem(f"relu_act_{n}")
        self.relu_dve = sem(f"relu_dve_{n}")
        self.down = sem(f"down_{n}")
        self.rows_out = sem(f"rows_out_{n}")
        self.kept = sem(f"kept_{n}")
        self.rows_loaded = [sem(f"rows_loaded{r}_{n}") for r in range(4)]
        self.rows_stored = [sem(f"rows_stored{r}_{n}") for r in range(4)]


def result_rows(shape, experts):
    B, L, D = shape
    return [B * L + (B * L + experts * (P - 1)) // P * P, D]


def macaron_block(nc, x_in, qkv_w, qkv_b, out_w, out_b, proj, centroids, ln_g, ln_b, w1, b1, w2, b2, out):
    B, L, D = x_in.shape
    H, HD, M = proj.shape
    E, _, F = w1.shape
    NT = B * L // P
    FC = F // P
    NS = (B * L + E * (P - 1)) // P
    NB = 4
    PAIRS = H // 2
    CHUNKS = L // P
    GROUPS = CHUNKS // NB
    assert D == P and F == 4 * P and H * HD == P and 2 * M == P and B * L % P == 0 and GROUPS == 2 and PAIRS == 8
    assert NS % 4 == 3
    assert NT // NB == 4

    AGGR = 6

    W1, W2, B2, B1, GG, BB = 0, F, F + FC * P, F + FC * P + D, F + FC * P + D + FC, F + FC * P + D + FC + 1
    REC = BB + 1
    R_B1, R_G, R_B, R_C, R_QB, NR = 0, E * FC, E * FC + E, E * FC + 2 * E, E * FC + 3 * E, E * FC + 3 * E + 2

    XN, KEPT, HALF_ALPHA, ROW = 0, D, 2 * D, 2 * D + 1
    token_rows = nc.dram_tensor("token_rows", [NT * P, ROW], F32, kind="Internal").ap()
    x_rows = nc.dram_tensor("x_rows", [(NT + NS) * P, D], F32, kind="Internal").ap()

    ctx = ExitStack()
    with ctx:
        def sb(name, shape, dt=F32):
            return ctx.enter_context(nc.sbuf_tensor(name, shape, dt))

        def sem(name):
            return ctx.enter_context(nc.semaphore(name))

        psum = ctx.enter_context(nc.psum_tensor("psum", [P, 8, 512], F32))

        ident = sb("ident", [P, P])
        causal = sb("causal", [P, P])
        ones = sb("ones", [P, P])
        later = sb("later", [P, P])
        go_on = sb("go_on", [P, E, NT])
        head_block = sb("head_block", [P, H])
        first_rank = sb("first_rank", [P, E])
        tile_edges = sb("tile_edges", [P, NT])
        slots = sb("slots", [P, NS + 1])
        eps_col = sb("eps_col", [P, 1])
        warm = sb("warm", [P, 1])
        places = sb("places", [P, P])
        partition = sb("partition", [P, 1])
        spare_row = sb("spare_row", [P, NS + 1])
        rows = sb("rows", [NR, P])
        cols = sb("cols", [P, NR])
        records = sb("records", [P, E, REC])
        qkv_sb = sb("qkv_sb", [P, 3 * D])
        v_bias = sb("v_bias", [P, D])
        outw_sb = sb("outw_sb", [P, D])
        out_bias = sb("out_bias", [P, D])
        proj_sb = sb("proj_sb", [P, M])
        w_turned = sb("w_turned", [P, 2, P])
        b_feat = sb("b_feat", [P, PAIRS, 2])

        x_all = sb("x", [P, NB + NT + NB, D])
        x = x_all[:, NB:NB + NT, :]
        f_all = sb("f", [P, NB + NT, D])
        f = f_all[:, NB:NB + NT, :]
        xn = sb("xn", [P, NT, D])
        stats = sb("stats", [P, NT, 6])
        mv1 = sb("mv1", [P, 2, NT])
        halves = sb("halves", [P, 4, NB])
        stats_a = sb("stats_a", [P, NB, 6])
        mv_a = sb("mv_a", [P, 2, NB])
        dev_a = sb("dev_a", [P, NB])
        rstd_a = sb("rstd_a", [P, NB])
        stats_f = sb("stats_f", [P, NB, 6])
        mv_f = sb("mv_f", [P, 2, NB])
        dev_f = sb("dev_f", [P, NB])
        rstd_f = sb("rstd_f", [P, NB])
        shrunk_f = sb("shrunk_f", [P, NB])
        dev = sb("dev", [P, NT])
        rstd = sb("rstd", [P, NT])
        shrunk = sb("shrunk", [P, NT])
        var_b = sb("var_b", [P, NB + NT])
        dev_b = sb("dev_b", [P, NT])
        rstd_b = sb("rstd_b", [P, NT])
        best = sb("best", [P, NT])
        alpha = sb("alpha", [P, NT])
        is_best = sb("is_best", [P, NT, E])
        ranked = sb("ranked", [P, NT, E])
        best_rank = sb("best_rank", [P, NT])
        onehot = sb("onehot", [P, E, NT])
        over = sb("over", [P, E, NT])
        tiles_e = sb("tiles_e", [P, 1 + E])
        tiles_upto = sb("tiles_upto", [P, 1 + E])
        run = sb("run", [P, E, NT])
        rank_at = sb("rank_at", [P, E, NT])
        placed_at = sb("placed_at", [P, E, NT])
        chosen_at = sb("chosen_at", [P, E, NT])
        pos = sb("pos", [P, NT], I32)
        tile_place = sb("tile_place", [P, 2, NT], I32)
        source = sb("source", [P, NS + 1], I32)
        taken_row = sb("taken_row", [P, NS + 1])
        empty_row = sb("empty_row", [P, NS + 1])
        target = sb("target", [P, NS + 1], I32)
        passed = sb("passed", [P, NS + 1, E])
        owner_f = sb("owner_f", [P, NS + 1])
        owner = sb("owner", [P, NS + 1], I32)

        rec = sb("rec", [P, 4, REC])
        lnT = sb("lnT", [P, 2, P])
        hid = sb("hid", [P, 2, FC, P])
        half_alpha = sb("half_alpha", [P, 4])
        rows_out = sb("rows_out", [P, 4, D])

        xa = sb("xa", [P, NB, D])
        loop_space = rec[:, :, :].rearrange("p k r -> p (k r)")
        xaT = loop_space[:, 0:NB * P].rearrange("p (k t) -> p k t", t=P)
        v_raw = loop_space[:, NB * P:2 * NB * P].rearrange("p (k d) -> p k d", d=D)
        k_rows = loop_space[:, 2 * NB * P:(2 * NB + PAIRS) * P].rearrange("p (r m) -> p r m", m=P)
        xaT_high = sb("xaT_high", [P, NB, P], F32R)
        xaT_low = sb("xaT_low", [P, NB, P], F32R)
        w_high = sb("w_high", [P, 2, H * M], F32R)
        w_low = sb("w_low", [P, 2, H * M], F32R)
        qT = sb("qT", [P, PAIRS, NB * P])
        kT = sb("kT", [P, PAIRS, NB * P])
        kT_space = kT[:, :, :].rearrange("p r t -> p (r t)")
        proj_wide = kT_space[:, 0:H * M].rearrange("p (h m) -> p h m", m=M)
        kept = kT_space[:, H * M:H * M + NT * (D + 1)].rearrange("p (t w) -> p t w", w=D + 1)
        qT_space = qT[:, :, :].rearrange("p r t -> p (r t)")
        f_turned = qT_space[:, 0:NT * P].rearrange("p (t q) -> p t q", q=P)
        rows_in = qT_space[:, NT * P:NT * P + 4 * ROW].rearrange("p (k w) -> p k w", w=ROW)
        base = qT_space[:, NT * P + 4 * ROW:NT * P + 4 * (ROW + D)].rearrange("p (k w) -> p k w", w=D)
        v_pair = sb("v_pair", [P, GROUPS, NB, PAIRS, 32])
        v_head = sb("v_head", [P, GROUPS, NB, PAIRS, 2, 32])
        scores = sb("scores", [P, 2, 4, NB, P])
        hot = scores[:, :, :, :, :].rearrange("p a b c d -> p (a b c d)").bitcast(BF16)
        place_hot = hot[:, 0:NT * P].rearrange("p (t k) -> p t k", k=P)
        tile_hot = hot[:, NT * P:NT * (P + 3 * (NS + 1))].rearrange("p (t a s) -> p t a s", a=3, s=NS + 1)
        o_sb = sb("o_sb", [P, 2, P])
        den = sb("den", [P, PAIRS, 2])
        inv_den = sb("inv_den", [P, PAIRS, 2])
        heads_out = sb("heads_out", [P, PAIRS, 2, HD])
        heads_T = sb("heads_T", [P, P])
        proj_out = sb("proj_out", [P, D])
        stateT = sb("stateT", [P, 2, P])
        state = sb("state", [P, PAIRS, 32])

        new_x_loaded = [sem(f"new_x_loaded{q}") for q in range(NT // NB)]
        x_loaded = [sem(f"x_loaded{q}") for q in range(NT // NB)]
        small_loaded = sem("small_loaded")
        attn_loaded = sem("attn_loaded")
        experts_loaded = sem("experts_loaded")
        filled = sem("filled")
        consts = sem("consts")
        cols_psum = sem("cols_psum")
        cols_ready = sem("cols_ready")
        records_ready = sem("records_ready")
        wide_ready = sem("wide_ready")
        w_turned_psum = sem("w_turned_psum")
        w_turned_sb = sem("w_turned_sb")
        w_feat_psum = sem("w_feat_psum")
        w_high_ready = sem("w_high_ready")
        w_low_ready = sem("w_low_ready")
        b_feat_ready = sem("b_feat_ready")
        x_high_ready = sem("x_high_ready")
        x_low_ready = sem("x_low_ready")
        b_feat_psum = sem("b_feat_psum")
        ffn = [FfnSignals(sem, n) for n in range(2)]
        a_stats, a_aggr, a_dev, a_rstd, a_norm = (sem(f"a_{s}") for s in ("stats", "aggr", "dev", "rstd", "norm"))
        wide_done = sem("wide_done")
        wide_read = sem("wide_read")
        v_ready = sem("v_ready")
        scored = sem("scored")
        masked = sem("masked")
        o_done = sem("o_done")
        o_read = sem("o_read")
        o_turned = sem("o_turned")
        den_ready = sem("den_ready")
        inv_ready = sem("inv_ready")
        heads_ready = sem("heads_ready")
        heads_turned = sem("heads_turned")
        heads_T_ready = sem("heads_T_ready")
        projected = sem("projected")
        projected_sb = sem("projected_sb")
        residual = sem("residual")
        stateT_done = sem("stateT_done")
        stateT_added = sem("stateT_added")
        state_turned = sem("state_turned")
        state_ready = sem("state_ready")

        block = ctx.enter_context(nc.Block())

        def ring(o):
            return (1 + o) % 4

        def ring_value(i, o):
            return i * 4 + (12 + 16 * ((o + 1) // 4))

        def early(i, o, n):
            return isinstance(i, int) and i + o < n

        LOOP_FROM, LOOP_TO = 5, NS - 2

        WIDE_G = 2 + 2 * PAIRS + 2 * NB
        WIDE_B = GROUPS * WIDE_G - 2
        KEY_ROWS = 1 + 2 * PAIRS

        def wide(b, g, idx):
            return b * WIDE_B + (1 + WIDE_G * g + idx)

        FEATURE_BANKS = 6

        def wide_bank(idx):
            if 1 <= idx <= 2 * PAIRS:
                return (idx + 3) % FEATURE_BANKS
            return (1 + idx) % 2

        def turn_idx(g):
            return WIDE_G - 1 if g < GROUPS - 1 else WIDE_G - 3

        @block.sync
        def _(sp):
            for q in range(NT // NB):
                sp.dma_start(x[:, q * NB:(q + 1) * NB, :],
                             x_in.rearrange("b (t p) d -> p (b t) d", p=P)[:, q * NB:(q + 1) * NB, :]
                             ).then_inc(x_loaded[q], 16)
            sp.wait_ge(small_loaded, 80)
            sp.dma_start(records[:, :, W1:W1 + F], w1.rearrange("e d f -> d e f")).then_inc(experts_loaded, 16)
            sp.dma_start(qkv_sb[:, :], qkv_w).then_inc(attn_loaded, 16)
            sp.dma_start(proj_sb[:, :], proj.rearrange("h d m -> (h d) m")).then_inc(attn_loaded, 16)
            for c in range(FC):
                sp.dma_start(records[:, :, W2 + c * D:W2 + (c + 1) * D],
                              w2[:, c * P:(c + 1) * P, :].rearrange("e p d -> p e d")).then_inc(experts_loaded, 16)
            sp.dma_start(records[:, :, B2:B2 + D],
                          b2.rearrange("(o e) d -> o e d", o=1).broadcast_to([P, E, D])).then_inc(experts_loaded, 16)
            sp.dma_start(v_bias[:, :], qkv_b.rearrange("(a d) -> a d", d=D)[2:3, :].broadcast_to([P, D])
                          ).then_inc(attn_loaded, 16)
            sp.dma_start(outw_sb[:, :], out_w).then_inc(attn_loaded, 16)
            sp.dma_start(out_bias[:, :], out_b.rearrange("(a d) -> a d", a=1).broadcast_to([P, D])
                          ).then_inc(attn_loaded, 16)
            for n in range(2):
                s = ffn[n]
                by_tile = token_rows.rearrange("(t p) w -> p t w", p=P)
                for q in range(NT // NB):
                    at = slice(q * NB, (q + 1) * NB)
                    sp.wait_ge(s.norm2, NB * (q + 1))
                    sp.dma_start(by_tile[:, at, XN:XN + D], xn[:, at, :]).then_inc(s.token_rows, 16)
                    if q == 1:
                        sp.wait_ge(s.kept, NT // NB + 1)
                        for half in range(2):
                            at = slice(half * NT // 2, (half + 1) * NT // 2)
                            sp.dma_start(by_tile[:, at, KEPT:ROW], kept[:, at, :]).then_inc(s.token_rows, 16)
                for o in range(-2, 2):
                    sp.wait_ge(s.rows_stored[ring(o)], ring_value(LOOP_TO, o))
                if n == 0:
                    for q in range(NT // NB):
                        sp.dma_start(x[:, q * NB:(q + 1) * NB, :],
                                     x_rows.rearrange("(t p) d -> p t d", p=P)[:, q * NB:(q + 1) * NB, :]
                                     ).then_inc(new_x_loaded[q], 16)

        @block.gpsimd
        def _(pool):
            fills = [(ident, 0.0), (later, -1.0), (causal, 1.0), (ones, 1.0), (head_block, 1.0)]
            for n, (t, value) in enumerate(fills):
                nc.gpsimd.memset(t[:, :], value).then_inc(filled, 1)
            nc.gpsimd.memset(eps_col[:, :], LN_EPS).then_inc(filled, 1)
            nc.gpsimd.memset(go_on[:, :, :], 1.0).then_inc(filled, 1)
            nc.gpsimd.memset(tiles_e[:, 0:1], 0.0).then_inc(filled, 1)
            pool.wait_ge(filled, 8)
            nc.gpsimd.memset(go_on[:, :, 0:1], 0.0).then_inc(filled, 1)
            nc.gpsimd.affine_select(out=ident[:, :], in_=ident[:, :], compare_op=ALU.not_equal, fill=1.0, base=0,
                                    pattern=[[-1, P]], channel_multiplier=1).then_inc(consts, 1)
            nc.gpsimd.affine_select(out=later[:, :], in_=later[:, :], compare_op=ALU.is_ge, fill=0.0, base=0,
                                    pattern=[[-1, P]], channel_multiplier=1).then_inc(consts, 1)
            nc.gpsimd.affine_select(out=causal[:, :], in_=causal[:, :], compare_op=ALU.is_ge, fill=0.0, base=0,
                                    pattern=[[1, P]], channel_multiplier=-1).then_inc(consts, 1)
            nc.gpsimd.iota(first_rank[:, :], pattern=[[-1, E]], base=E, channel_multiplier=0,
                           allow_small_or_imprecise_dtypes=True).then_inc(consts, 1)
            nc.gpsimd.iota(tile_edges[:, :], pattern=[[P, NT]], base=0, channel_multiplier=0,
                           allow_small_or_imprecise_dtypes=True).then_inc(consts, 1)
            nc.gpsimd.iota(slots[:, :], pattern=[[1, NS + 1]], base=0, channel_multiplier=0,
                           allow_small_or_imprecise_dtypes=True).then_inc(consts, 1)
            nc.gpsimd.iota(places[:, :], pattern=[[1, P]], base=0, channel_multiplier=0,
                           allow_small_or_imprecise_dtypes=True).then_inc(consts, 1)
            nc.gpsimd.iota(partition[:, :], pattern=[[0, 1]], base=0, channel_multiplier=1,
                           allow_small_or_imprecise_dtypes=True).then_inc(consts, 1)
            nc.gpsimd.iota(spare_row[:, :], pattern=[[P, NS + 1]], base=NT * P, channel_multiplier=1,
                           allow_small_or_imprecise_dtypes=True).then_inc(consts, 1)
            nc.gpsimd.affine_select(out=head_block[:, :], in_=head_block[:, :], compare_op=ALU.is_ge, fill=0.0,
                                    base=0, pattern=[[-HD, H]], channel_multiplier=1).then_inc(consts, 1)
            pool.wait_ge(consts, 10)
            nc.gpsimd.affine_select(out=head_block[:, :], in_=head_block[:, :], compare_op=ALU.is_ge, fill=0.0,
                                    base=HD - 1, pattern=[[HD, H]], channel_multiplier=-1).then_inc(consts, 1)
            nc.gpsimd.memset(x_all[:, 0:NB, :], 0.0).then_inc(filled, 1)
            nc.gpsimd.memset(x_all[:, NB + NT:NB + NT + NB, :], 0.0).then_inc(filled, 1)
            nc.gpsimd.memset(v_pair[:, :, :, :, :], 0.0).then_inc(filled, 1)
            nc.gpsimd.memset(v_head[:, :, :, :, :, :], 0.0).then_inc(filled, 1)
            pool.wait_ge(filled, 13)
            for g in range(GROUPS):
                for a in range(2):
                    nc.gpsimd.memset(v_pair[:, g, :, :, 9 * a + HD:9 * a + HD + 1], 1.0).then_inc(filled, 1)
                    nc.gpsimd.memset(v_head[:, g, :, :, a, 9 * a + HD:9 * a + HD + 1], 1.0).then_inc(filled, 1)
            pool.wait_ge(cols_ready, 1)
            nc.gpsimd.tensor_copy(records[:, :, B1:B1 + FC],
                                  cols[:, R_B1:R_B1 + E * FC].rearrange("p (e c) -> p e c", c=FC)
                                  ).then_inc(records_ready, 1)
            nc.gpsimd.tensor_copy(records[:, :, GG:GG + 1],
                                  cols[:, R_G:R_G + E].rearrange("p (e c) -> p e c", c=1)).then_inc(records_ready, 1)
            nc.gpsimd.tensor_copy(records[:, :, BB:BB + 1],
                                  cols[:, R_B:R_B + E].rearrange("p (e c) -> p e c", c=1)).then_inc(records_ready, 1)

            for n in range(2):
                s = ffn[n]
                if n == 1:
                    with pool.Fori(0, B) as b:
                        for g in range(GROUPS):
                            pool.wait_ge(wide_read, b * WIDE_B + (2 + WIDE_G * g))
                            src = v_raw[:, :, :].rearrange("p k (r a d) -> p k r a d", a=2, d=HD)
                            bias = v_bias[:, :].rearrange("p (r a d) -> p r a d", a=2, d=HD)
                            for k in range(NB):
                                nc.gpsimd.tensor_tensor(
                                    v_pair[:, g, k, :, 0:18].rearrange("p r (a d) -> p r a d", a=2)[:, :, :, 0:HD],
                                    src[:, k], bias, ALU.add).then_inc(v_ready, 1)
                                flat = v_head[:, g, k, :, :, :].rearrange("p r a w -> p r (a w)")
                                for a in range(2):
                                    nc.gpsimd.tensor_tensor(flat[:, :, 41 * a:41 * a + HD], src[:, k, :, a, :],
                                                            bias[:, :, a, :], ALU.add).then_inc(v_ready, 1)

                pool.wait_ge(s.token_rows, 16 * (NT // NB + 2))
                pool.wait_ge(s.sources, 1)
                AHEAD = 4
                for j in range(-AHEAD, NS):
                    m = j + AHEAD
                    if m < NS:
                        if m >= 4:
                            pool.wait_ge(s.inputs, 3 * (m - 3))
                        pool.indirect_dma_start(
                            out=rows_in[:, m % 4, :], out_offset=None, in_=token_rows[:, :],
                            in_offset=bass.IndirectOffsetOnAxis(ap=source[:, m:m + 1], axis=0)
                            ).then_inc(s.rows_loaded[m % 4], 16)
                    if j == 0:
                        pool.wait_ge(s.targets, 1)
                    if j >= 0:
                        pool.wait_ge(s.rows_out, j + 1)
                        pool.indirect_dma_start(
                            out=(x_rows, out)[n][:, :], out_offset=bass.IndirectOffsetOnAxis(ap=target[:, j:j + 1], axis=0),
                            in_=rows_out[:, j % 4, :], in_offset=None).then_inc(s.rows_stored[j % 4], 16)

        @block.scalar
        def _(act):
            act.dma_start(rows[R_B1:R_B1 + E * FC, :], b1.rearrange("e (c p) -> (e c) p", p=P)
                          ).then_inc(small_loaded, 16)
            act.dma_start(rows[R_G:R_G + E, :], ln_g).then_inc(small_loaded, 16)
            act.dma_start(rows[R_B:R_B + E, :], ln_b).then_inc(small_loaded, 16)
            act.dma_start(rows[R_C:R_C + E, :], centroids).then_inc(small_loaded, 16)
            act.dma_start(rows[R_QB:R_QB + 2, :], qkv_b.rearrange("(a d) -> a d", d=D)[0:2, :]
                          ).then_inc(small_loaded, 16)
            def deviation(out_ap, var_ap, signal):
                nc.scalar.activation(out_ap, var_ap, ACT.Sqrt, bias=eps_col[:, 0:1]).then_inc(signal, 1)

            def blocks(q):
                return slice(q * NB, (q + 1) * NB)

            act.wait_ge(filled, 6)
            nc.scalar.activation(warm[:, :], eps_col[:, :], ACT.Sqrt)
            for n in range(2):
                s = ffn[n]
                for step in range(NT // NB + 1):
                    if n == 0 and step < NT // NB:
                        act.wait_ge(s.aggr1, AGGR * (step + 1))
                        deviation(dev[:, blocks(step)], mv1[:, 1, blocks(step)], s.dev1)
                    q = step - 1
                    if q >= 0:
                        act.wait_ge(s.f_turned, q + 1)
                        nc.scalar.activation(f_turned[:, blocks(q), :], psum[:, q % 2, :], ACT.Copy
                                             ).then_inc(s.f_turned_sb, 1)
                    if n == 1 and step == NT // NB - 1:
                        act.wait_ge(s.aggr1, AGGR * (NT // NB + 1))
                        deviation(dev_f[:, :], mv_f[:, 1, :], s.dev1)
                act.wait_ge(s.var2, 2 if n == 0 else 2 * (NT // NB + 1))
                deviation(dev_b[:, :], var_b[:, NB:NB + NT], s.dev2)
                act.wait_ge(s.rstd2, 1)
                for t in range(NT):
                    nc.scalar.activation(xn[:, t, :], f[:, t, :], ACT.Copy, scale=rstd_b[:, t:t + 1]
                                         ).then_inc(s.norm2, 1)
                    if t == NB - 1:
                        act.wait_ge(s.route, 1)
                        nc.scalar.activation(alpha[:, :], best[:, :], ACT.Sigmoid).then_inc(s.gate, 1)

                def relu(i, o, par):
                    act.wait_ge(s.up, 2 * (i + o) + 1)
                    for c in range(FC // 2):
                        nc.scalar.activation(hid[:, par, c, :], psum[:, 4 + 2 * par, c * P:(c + 1) * P], ACT.Relu,
                                             bias=rec[:, ring(o), B1 + c:B1 + c + 1]).then_inc(s.relu_act, 1)

                def fetch(i, o):
                    at = act.value_load(owner[0:1, bass.ds(i + o, 1)], min_val=0, max_val=(E - 1) * REC)
                    if not early(i, o, 4):
                        act.wait_ge(s.rows_out, i + (o - 3))
                    flat = records[:, :, :].rearrange("p e r -> p (e r)")
                    nc.scalar.activation(rec[:, ring(o), :], flat[:, bass.ds(at, REC)], ACT.Copy
                                         ).then_inc(s.weights, 1)

                if n == 0:
                    act.wait_ge(experts_loaded, 16 * (2 + FC))
                    act.wait_ge(records_ready, 3)
                act.wait_ge(s.table, 1)
                for o in range(-1, 1):
                    fetch(1, o)
                for o in range(-1, 4):
                    fetch(1, o + 2)
                    relu(1, o, (1 + o) % 2)
                with act.Fori(LOOP_FROM, LOOP_TO - 3, 4) as i:
                    for o in range(4):
                        fetch(i, o + 2)
                        relu(i, o, (1 + o) % 2)
                for o in range(2):
                    relu(LOOP_TO, o, (1 + o) % 2)

                if n == 1:
                    continue
                act.wait_ge(s.rows_out, NS)
                act.wait_ge(w_turned_psum, 1)
                nc.scalar.activation(w_turned[:, :, :], psum[:, 4, 0:2 * P], ACT.Copy).then_inc(w_turned_sb, 1)
                for j in range(4):
                    act.wait_ge(w_feat_psum, j + 1)
                    nc.scalar.activation(w_high[:, j // 2, (j % 2) * 512:(j % 2 + 1) * 512],
                                         psum[:, 4 + j, :], ACT.Copy).then_inc(w_high_ready, 1)
                act.wait_ge(b_feat_psum, 1)
                nc.scalar.activation(b_feat[:, :, :], psum[:, 1, 0:2 * PAIRS], ACT.Copy).then_inc(b_feat_ready, 1)
                act.wait_ge(a_aggr, AGGR)
                deviation(dev_a[:, :], mv_a[:, 1, :], a_dev)
                act.wait_ge(wide_done, 1)
                nc.scalar.activation(xaT[:, :, :], psum[:, 0, :], ACT.Copy).then_inc(wide_read, 1)
                nc.scalar.activation(xaT_high[:, :, :], psum[:, 0, :], ACT.Copy).then_inc(x_high_ready, 1)

                def keys_rows(b, g, k):
                    if (g, k) != (0, 0):
                        act.wait_ge(stateT_done, b * (CHUNKS - 1) + (NB * g + k))
                    for h in range(2):
                        idx = KEY_ROWS + 2 * k + h
                        act.wait_ge(wide_done, wide(b, g, idx) + 1)
                        nc.scalar.activation(k_rows[:, 4 * h:4 * h + 4, :], psum[:, wide_bank(idx), :], ACT.Copy
                                             ).then_inc(wide_read, 1)

                def heads_turn(b, c):
                    act.wait_ge(heads_turned, b * CHUNKS + (c + 1))
                    nc.scalar.activation(heads_T[:, :], psum[:, 6, 0:P], ACT.Copy).then_inc(heads_T_ready, 1)

                act.wait_ge(b_feat_ready, 1)
                with act.Fori(0, B) as b:
                    for g in range(GROUPS):
                        act.wait_ge(wide_done, wide(b, g, 0) + 1)
                        nc.scalar.activation(v_raw[:, :, :], psum[:, 1, :], ACT.Copy).then_inc(wide_read, 1)
                        for r in range(PAIRS):
                            for a, dst in ((0, qT), (1, kT)):
                                idx = 1 + 2 * r + a
                                act.wait_ge(wide_done, wide(b, g, idx) + 1)
                                nc.scalar.activation(dst[:, r, :], psum[:, wide_bank(idx), :], ACT.Relu,
                                                     bias=b_feat[:, r, a:a + 1]).then_inc(wide_read, 1)
                                if g == 1 and idx == 6:
                                    heads_turn(b, NB * g - 1)
                        act.wait_ge(ffn[1].aggr1, b * (AGGR * GROUPS) + AGGR * (g + 1))
                        deviation(dev_f[:, :], mv_f[:, 1, :], ffn[1].dev1)
                        for k in range(NB):
                            c = NB * g + k
                            if c < CHUNKS - 1:
                                keys_rows(b, g, k)
                            if k == NB - 1:
                                idx = turn_idx(g)
                                act.wait_ge(wide_done, wide(b, g, idx) + 1)
                                nc.scalar.activation(xaT[:, :, :], psum[:, wide_bank(idx), :], ACT.Copy
                                                     ).then_inc(wide_read, 1)
                                nc.scalar.activation(xaT_high[:, :, :], psum[:, wide_bank(idx), :], ACT.Copy
                                                     ).then_inc(x_high_ready, 1)
                            act.wait_ge(o_done, b * CHUNKS + (c + 1))
                            nc.scalar.activation(o_sb[:, :, :], psum[:, 6, 0:2 * P], ACT.Copy).then_inc(o_read, 1)
                            if k == 1:
                                act.wait_ge(a_aggr, b * (AGGR * GROUPS) + AGGR * (g + 2))
                                deviation(dev_a[:, :], mv_a[:, 1, :], a_dev)
                            if k < NB - 1 or g == GROUPS - 1:
                                heads_turn(b, c)

        @block.tensor
        def _(pe):
            def turn(bank, at, src):
                return nc.tensor.transpose(psum[:, bank, at:at + src.shape[0]], src, ident[0:src.shape[0], 0:src.shape[0]])

            def stay_warm(count):
                for _ in range(count):
                    nc.tensor.matmul(psum[:, 7, 0:P], ident[:, :], ident[:, :], start=True, stop=True)

            pe.wait_ge(consts, 1)
            stay_warm(6)
            pe.wait_ge(small_loaded, 80)
            nc.tensor.transpose(psum[:, 3, 0:NR], rows[:, :], ident[0:NR, 0:NR]).then_inc(cols_psum, 1)

            for n in range(2):
                s = ffn[n]
                def turn_f(q):
                    pe.wait_ge(s.norm1, NB * (q + 1 + n))
                    if q >= 2:
                        pe.wait_ge(s.f_turned_sb, q - 1)
                    for t in range(NB):
                        last = turn(q % 2, t * P, f[:, q * NB + t, :])
                    last.then_inc(s.f_turned, 1)

                def affinity(q):
                    pe.wait_ge(s.f_turned_sb, q + 1)
                    if n == 0 and q == 0:
                        pe.wait_ge(cols_ready, 1)
                    for t in range(q * NB, (q + 1) * NB):
                        last = nc.tensor.matmul(psum[:, 2, t * E:(t + 1) * E], f_turned[:, t, :],
                                                cols[:, R_C:R_C + E], start=True, stop=True)
                    return last

                turn_f(0)
                for q in range(1, NT // NB):
                    if n == 0 or q == 3:
                        affinity(q - 1)
                        turn_f(q)
                    else:
                        turn_f(q)
                        affinity(q - 1)
                last = affinity(NT // NB - 1)
                last.then_inc(s.affinity, 1)
                stay_warm(6)
                if n == 0:
                    pe.wait_ge(consts, 11)
                pe.wait_ge(s.onehot, 1)
                hot = onehot[:, :, :].rearrange("p e t -> p (e t)")
                nc.tensor.matmul(psum[:, 3, 0:E * NT], later[:, :], hot, start=True, stop=True)
                nc.tensor.matmul(psum[:, 3, E * NT:2 * E * NT], ones[:, :], hot, start=True, stop=True
                                 ).then_inc(s.counts, 1)
                stay_warm(14)

                for q in range(NT // NB):
                    pe.wait_ge(s.place_hot, q + 1)
                    for t in range(q * NB, (q + 1) * NB):
                        last = nc.tensor.matmul(psum[:, 2, 0:3 * (NS + 1)], place_hot[:, t, :],
                                                tile_hot[:, t, :, :].rearrange("p a s -> p (a s)"),
                                                start=(t == 0), stop=(t == NT - 1))
                last.then_inc(s.inverse, 1)
                stay_warm(8)
                def turn_rows(i, o, par):
                    pe.wait_ge(s.rows_loaded[ring(o)], ring_value(i, o))
                    turn(par, 0, rows_in[:, ring(o), XN:XN + D]).then_inc(s.rows_turned, 1)

                def up(i, o, par):
                    pe.wait_ge(s.inputs, 3 * i + (3 * o + 1))
                    for c in range(FC):
                        last = nc.tensor.matmul(psum[:, 4 + 2 * par + c // 2, (c % 2) * P:(c % 2 + 1) * P],
                                                rec[:, ring(o), W1 + c * P:W1 + (c + 1) * P], lnT[:, par, :],
                                                start=True, stop=True)
                        if c % 2:
                            last.then_inc(s.up, 1)

                def down(i, o, par):
                    pe.wait_ge(s.relu_act, 2 * (i + o) + 2)
                    pe.wait_ge(s.relu_dve, 2 * (i + o) + 2)
                    for c in range(FC):
                        last = nc.tensor.matmul(psum[:, 2 + par, 0:D], hid[:, par, c, :],
                                                rec[:, ring(o), W2 + c * D:W2 + (c + 1) * D],
                                                start=(c == 0), stop=(c == FC - 1))
                    last.then_inc(s.down, 1)

                def tile_step(i, o):
                    up(i, o, (1 + o) % 2)
                    if not (isinstance(i, int) and i + o == NS - 1):
                        turn_rows(i, o + 1, o % 2)
                    if not early(i, o, 1):
                        down(i, o - 1, o % 2)

                pe.wait_ge(s.targets, 1)
                turn_rows(1, -1, 0)
                for o in range(-1, 4):
                    tile_step(1, o)
                with pe.Fori(LOOP_FROM, LOOP_TO - 3, 4) as i:
                    for o in range(4):
                        tile_step(i, o)
                for o in range(2):
                    tile_step(LOOP_TO, o)
                down(LOOP_TO, 1, 0)

                if n == 1:
                    continue
                pe.wait_ge(attn_loaded, 80)
                for a in range(2):
                    last = turn(4, a * P, qkv_sb[:, a * D:(a + 1) * D])
                last.then_inc(w_turned_psum, 1)
                pe.wait_ge(w_turned_sb, 1)
                pe.wait_ge(wide_ready, 1)
                wide_flat = proj_wide[:, :, :].rearrange("p h m -> p (h m)")
                for j in range(4):
                    nc.tensor.matmul(psum[:, 4 + j, :], w_turned[:, j // 2, :],
                                     wide_flat[:, (j % 2) * 512:(j % 2 + 1) * 512], start=True, stop=True
                                     ).then_inc(w_feat_psum, 1)
                for r in range(PAIRS):
                    last = nc.tensor.matmul(psum[:, 1, 2 * r:2 * r + 2], wide_flat[:, r * P:(r + 1) * P],
                                            cols[:, R_QB:R_QB + 2], start=True, stop=True)
                last.then_inc(b_feat_psum, 1)
                pe.wait_ge(b_feat_ready, 1)
                pe.wait_ge(w_low_ready, 4)
                stay_warm(18)
                pe.wait_ge(a_norm, NB)
                for t in range(NB):
                    last = turn(0, t * P, xa[:, t, :])
                last.then_inc(wide_done, 1)

                def values(b, g):
                    pe.wait_ge(wide_read, wide(b, g, 0))
                    for k in range(NB):
                        last = nc.tensor.matmul(psum[:, 1, k * P:(k + 1) * P], xaT[:, k, :], qkv_sb[:, 2 * D:3 * D],
                                                start=True, stop=True)
                    last.then_inc(wide_done, 1)

                def features(b, g, r):
                    if r == 0:
                        pe.wait_ge(x_low_ready, b * GROUPS + (g + 1))
                    for a in range(2):
                        idx = 1 + 2 * r + a
                        if idx == 3:
                            pe.wait_ge(wide_read, wide(b, g, 0) + 1)
                        if a == 0 and idx > FEATURE_BANKS:
                            pe.wait_ge(wide_read, wide(b, g, idx + 1 - FEATURE_BANKS) + 1)
                        parts = ((w_high, xaT_high), (w_low, xaT_high), (w_high, xaT_low))
                        for u, (w_part, x_part) in enumerate(parts):
                            last = nc.tensor.matmul(psum[:, wide_bank(idx), :], w_part[:, a, r * P:(r + 1) * P],
                                                    x_part[:, :, :].rearrange("p k t -> p (k t)"),
                                                    start=(u == 0), stop=(u == 2))
                        last.then_inc(wide_done, 1)

                def score(g, k, half):
                    at = slice(k * P, (k + 1) * P)
                    for r in range(4):
                        for a in range(2):
                            last = nc.tensor.matmul(psum[:, 2 + 2 * half + a, r * P:(r + 1) * P],
                                                    kT[64 * a:64 * a + 64, 4 * half + r, at],
                                                    qT[64 * a:64 * a + 64, 4 * half + r, at], start=True, stop=True)
                            if r == 3:
                                last.then_inc(scored, 1)

                def key_rows(b, g, k, h):
                    idx = KEY_ROWS + 2 * k + h
                    pe.wait_ge(wide_read, wide(b, g, idx) - 1)
                    for r in range(4):
                        last = turn(wide_bank(idx), r * P, kT[:, 4 * h + r, k * P:(k + 1) * P])
                    last.then_inc(wide_done, 1)

                def turn_next(b, g):
                    idx = turn_idx(g)
                    pe.wait_ge(wide_read, wide(b, g, idx) - 1)
                    pe.wait_ge(a_norm, b * (NB * GROUPS) + NB * (g + 2))
                    for t in range(NB):
                        last = turn(wide_bank(idx), t * P, xa[:, t, :])
                    last.then_inc(wide_done, 1)

                def context(b, g, k):
                    c = NB * g + k
                    pe.wait_ge(state_ready, b * CHUNKS + (c + 1))
                    if c > 0:
                        pe.wait_ge(projected_sb, b * CHUNKS + c)
                    for half in range(2):
                        for r in range(4):
                            nc.tensor.matmul(psum[32 * r:32 * r + 32, 6, half * P:(half + 1) * P],
                                             state[:, 4 * half + r, :], qT[:, 4 * half + r, k * P:(k + 1) * P],
                                             start=(half == 0), stop=False, skip_group_check=True)
                    if k == 0:
                        pe.wait_ge(v_ready, b * (3 * CHUNKS) + 3 * NB * (g + 1))
                    for half in range(2):
                        for a in range(2):
                            if half == 1:
                                pe.wait_ge(masked, b * (4 * CHUNKS) + (4 * c + 3 + a))
                            elif a == 0:
                                pe.wait_ge(masked, b * (4 * CHUNKS) + (4 * c + 2))
                            for r in range(4):
                                last = nc.tensor.matmul(psum[32 * r:32 * r + 32, 6, half * P:(half + 1) * P],
                                                        v_head[:, g, k, 4 * half + r, a, :],
                                                        scores[:, k % 2, 2 * half + a, r, :],
                                                        start=False, stop=(half == 1 and a == 1),
                                                        skip_group_check=True)
                    last.then_inc(o_done, 1)

                def turn_context(b, c):
                    pe.wait_ge(o_read, b * CHUNKS + (c + 1))
                    for half in range(2):
                        last = turn(6, half * P, o_sb[:, half, :])
                    last.then_inc(o_turned, 1)

                def state_sums(b, g, k):
                    pe.wait_ge(wide_read, wide(b, g, KEY_ROWS + 2 * k + 1) + 1)
                    for half in range(2):
                        for r in range(4):
                            last = nc.tensor.matmul(psum[32 * r:32 * r + 32, 7, half * P:(half + 1) * P],
                                                    v_pair[:, g, k, 4 * half + r, :], k_rows[:, 4 * half + r, :],
                                                    start=True, stop=True)
                    last.then_inc(stateT_done, 1)

                def turn_state(b, c):
                    pe.wait_ge(stateT_added, b * (CHUNKS - 1) + (c + 1))
                    for half in range(2):
                        last = turn(7, half * P, stateT[:, half, :])
                    last.then_inc(state_turned, 1)

                def turn_heads(b, c):
                    pe.wait_ge(heads_ready, b * CHUNKS + (c + 1))
                    turn(6, 0, heads_out[:, :, :, :].rearrange("p r a d -> p (r a d)")).then_inc(heads_turned, 1)

                def project(b, c):
                    pe.wait_ge(heads_T_ready, b * CHUNKS + (c + 1))
                    nc.tensor.matmul(psum[:, 6, 0:D], heads_T[:, :], outw_sb[:, :], start=True, stop=True
                                     ).then_inc(projected, 1)

                with pe.Fori(0, B) as b:
                    for g in range(GROUPS):
                        values(b, g)
                        for r in range(PAIRS):
                            features(b, g, r)
                            if g > 0:
                                if r == 0:
                                    turn_context(b, NB * g - 1)
                                    state_sums(b, g - 1, NB - 1)
                                if r == 1:
                                    turn_heads(b, NB * g - 1)
                                    turn_state(b, NB * g - 1)
                                if r == 4:
                                    project(b, NB * g - 1)
                        pe.wait_ge(wide_read, wide(b, g, 12) + 1)
                        score(g, 0, 0)
                        pe.wait_ge(wide_read, wide(b, g, 2 * PAIRS) + 1)
                        score(g, 0, 1)
                        for k in range(NB):
                            c = NB * g + k
                            if c < CHUNKS - 1:
                                if k == 0:
                                    key_rows(b, g, k, 0)
                                key_rows(b, g, k, 1)
                            if k == NB - 1:
                                turn_next(b, g)
                            context(b, g, k)
                            if k < NB - 1:
                                score(g, k + 1, 0)
                                turn_context(b, c)
                                state_sums(b, g, k)
                                score(g, k + 1, 1)
                                turn_heads(b, c)
                                turn_state(b, c)
                                if c + 1 < CHUNKS - 1:
                                    key_rows(b, g, k + 1, 0)
                                project(b, c)
                            elif g == GROUPS - 1:
                                turn_context(b, c)
                                turn_heads(b, c)
                                project(b, c)

        @block.vector
        def _(dve):
            def norm_stats(source, stats_to, mv, stats_signal, aggr_signal, blocks_before):
                for k in range(NB):
                    nc.vector.bn_stats(stats_to[:, k, :], source(k)).then_inc(stats_signal, 1)
                steps = blocks_before * AGGR
                dve.wait_ge(stats_signal, (blocks_before + 1) * NB)
                nc.vector.tensor_tensor(halves[:, 0, :], stats_to[:, :, 1], stats_to[:, :, 4], ALU.add
                                        ).then_inc(aggr_signal, 1)
                nc.vector.tensor_tensor(halves[:, 1, :], stats_to[:, :, 1], stats_to[:, :, 4], ALU.subtract
                                        ).then_inc(aggr_signal, 1)
                nc.vector.tensor_tensor(halves[:, 2, :], stats_to[:, :, 2], stats_to[:, :, 5], ALU.add
                                        ).then_inc(aggr_signal, 1)
                dve.wait_ge(aggr_signal, steps + 3)
                nc.vector.scalar_tensor_tensor(out=halves[:, 3, :], in0=halves[:, 1, :], scalar=0.25,
                                               in1=halves[:, 1, :], op0=ALU.mult, op1=ALU.mult
                                               ).then_inc(aggr_signal, 1)
                nc.vector.tensor_scalar(mv[:, 0, :], halves[:, 0, :], 0.5, None, ALU.mult).then_inc(aggr_signal, 1)
                dve.wait_ge(aggr_signal, steps + 5)
                nc.vector.scalar_tensor_tensor(out=mv[:, 1, :], in0=halves[:, 2, :], scalar=1.0 / D,
                                               in1=halves[:, 3, :], op0=ALU.mult, op1=ALU.add
                                               ).then_inc(aggr_signal, 1)

            def norm_apply(source, dest, mv, dev_, rstd_, dev_signal, rstd_signal, norm_signal, blocks_before):
                dve.wait_ge(dev_signal, blocks_before + 1)
                nc.vector.reciprocal(rstd_, dev_).then_inc(rstd_signal, 1)
                dve.wait_ge(rstd_signal, blocks_before + 1)
                for k in range(NB):
                    nc.vector.tensor_scalar(dest(k), source(k), mv[:, 0, k:k + 1], rstd_[:, k:k + 1],
                                            ALU.subtract, ALU.mult).then_inc(norm_signal, 1)

            def tiles_of(data, first):
                return lambda k: data[:, bass.ds(first + k, 1), :].squeeze(1)

            def variance_of_normed(to, shrunk_, var, rstd_, signal, blocks_before):
                nc.vector.tensor_tensor(shrunk_, var, rstd_, ALU.mult).then_inc(signal, 1)
                dve.wait_ge(signal, blocks_before * 2 + 1)
                nc.vector.tensor_tensor(to, shrunk_, rstd_, ALU.mult).then_inc(signal, 1)

            def second_stats(blocks_before):
                norm_stats(tiles_of(x_all, blocks_before * NB), stats_f, mv_f, ffn[1].stats1, ffn[1].aggr1,
                           blocks_before)

            def second_apply(blocks_before):
                norm_apply(tiles_of(x_all, blocks_before * NB), tiles_of(f_all, blocks_before * NB), mv_f,
                           dev_f[:, :], rstd_f[:, :], ffn[1].dev1, ffn[1].rstd1, ffn[1].norm1, blocks_before)
                variance_of_normed(var_b[:, bass.ds(blocks_before * NB, NB)], shrunk_f[:, :], mv_f[:, 1, :],
                                   rstd_f[:, :], ffn[1].var2, blocks_before)

            for n in range(2):
                s = ffn[n]
                if n == 0:
                    for step in range(NT // NB + 1):
                        if step < NT // NB:
                            q = slice(step * NB, (step + 1) * NB)
                            dve.wait_ge(x_loaded[step], 16)
                            norm_stats(tiles_of(x, step * NB), stats[:, q, :], mv1[:, :, q], s.stats1, s.aggr1, step)
                        if step == 1:
                            dve.wait_ge(cols_psum, 1)
                            nc.vector.tensor_copy(cols[:, :], psum[:, 3, 0:NR]).then_inc(cols_ready, 1)
                        if step > 0:
                            q = slice((step - 1) * NB, step * NB)
                            norm_apply(tiles_of(x, (step - 1) * NB), tiles_of(f, (step - 1) * NB), mv1[:, :, q],
                                       dev[:, q], rstd[:, q], s.dev1, s.rstd1, s.norm1, step - 1)
                    variance_of_normed(var_b[:, NB:NB + NT], shrunk[:, :], mv1[:, 1, :], rstd[:, :], s.var2, 0)
                else:
                    second_stats(NT // NB)
                    second_apply(NT // NB)

                dve.wait_ge(s.norm1, NT if n == 0 else NT + NB)
                for q in range(NT // NB):
                    at = slice(q * NB, (q + 1) * NB)
                    nc.vector.scalar_tensor_tensor(out=kept[:, at, 0:D], in0=f[:, at, :], scalar=0.5, in1=x[:, at, :],
                                                   op0=ALU.mult, op1=ALU.add).then_inc(s.kept, 1)

                route = [0]

                def link(ins, count=1):
                    route[0] += count
                    ins.then_inc(s.route, 1)
                    dve.wait_ge(s.route, route[0])

                def over_t(ap, width):
                    return ap.unsqueeze(2).broadcast_to([P, ap.shape[1], width])

                def over_first(ap, count):
                    return ap.unsqueeze(1).broadcast_to([P, count, ap.shape[1]])

                dve.wait_ge(s.dev2, 1)
                nc.vector.reciprocal(rstd_b[:, :], dev_b[:, :]).then_inc(s.rstd2, 1)
                dve.wait_ge(s.affinity, 1)
                if n == 0:
                    dve.wait_ge(consts, 11)
                aff = psum[:, 2, 0:NT * E].rearrange("p (t e) -> p t e", e=E)
                link(nc.vector.reduce_max(best[:, :], aff, AX_X))
                link(nc.vector.tensor_tensor(is_best[:, :, :], aff, over_t(best[:, :], E), ALU.is_ge))
                link(nc.vector.tensor_tensor(ranked[:, :, :], is_best[:, :, :], over_first(first_rank[:, :], NT), ALU.mult))
                link(nc.vector.reduce_max(best_rank[:, :], ranked[:, :, :], AX_X))
                nc.vector.tensor_tensor(onehot[:, :, :].rearrange("p e t -> p t e"), ranked[:, :, :],
                                        over_t(best_rank[:, :], E), ALU.is_equal).then_inc(s.onehot, 1)
                dve.wait_ge(s.gate, 1)
                nc.vector.tensor_scalar(kept[:, :, D], alpha[:, :], 0.5, None, ALU.mult).then_inc(s.kept, 1)
                dve.wait_ge(s.counts, 1)
                dve.wait_ge(s.onehot, 1)
                if n == 0:
                    dve.wait_ge(filled, 9)
                flat = lambda ap: ap.rearrange("p e t -> p (e t)")
                link(nc.vector.tensor_tensor_scan(flat(run[:, :, :]), flat(go_on[:, :, :]),
                                                  psum[:, 3, E * NT:2 * E * NT], 0.0, ALU.mult, ALU.add))
                link(nc.vector.tensor_tensor(over[:, :, :], over_t(run[:, :, NT - 1], NT),
                                             over_first(tile_edges[:, :], E), ALU.is_gt))
                nc.vector.reduce_sum(tiles_e[:, 1:1 + E], over[:, :, :], AX_X).then_inc(s.route, 1)
                link(nc.vector.tensor_tensor(flat(rank_at[:, :, :]), psum[:, 3, 0:E * NT], flat(run[:, :, :]),
                                             ALU.add), 2)
                link(nc.vector.tensor_tensor_scan(tiles_upto[:, :], ones[:, 0:1 + E], tiles_e[:, :], 0.0,
                                                  ALU.mult, ALU.add))
                link(nc.vector.scalar_tensor_tensor(out=placed_at[:, :, :], in0=over_t(tiles_upto[:, 0:E], NT),
                                                    scalar=float(P), in1=rank_at[:, :, :],
                                                    op0=ALU.mult, op1=ALU.add))
                link(nc.vector.tensor_tensor(chosen_at[:, :, :], placed_at[:, :, :], onehot[:, :, :], ALU.mult))
                with nc.allow_low_precision("whole numbers below 4096"):
                    link(nc.vector.reduce_sum(pos[:, :], chosen_at[:, :, :].rearrange("p e t -> p t e"), AX_X))
                nc.vector.tensor_scalar(tile_place[:, 0, :], pos[:, :], P.bit_length() - 1, None,
                                        ALU.logical_shift_right).then_inc(s.route, 1)
                link(nc.vector.tensor_scalar(tile_place[:, 1, :], pos[:, :], P - 1, None, ALU.bitwise_and), 2)
                link(nc.vector.tensor_tensor(tile_hot[:, :, 0, :], over_t(tile_place[:, 0, :], NS + 1),
                                             over_first(slots[:, :], NT), ALU.is_equal))
                nc.vector.tensor_scalar(tile_hot[:, :, 1, :], tile_hot[:, :, 0, :], partition[:, 0:1], None,
                                        ALU.mult)
                nc.vector.tensor_tensor(tile_hot[:, :, 2, :], tile_hot[:, :, 0, :],
                                        over_t(tile_edges[:, :], NS + 1), ALU.mult)
                for q in range(NT // NB):
                    nc.vector.tensor_tensor(place_hot[:, q * NB:(q + 1) * NB, :], over_first(places[:, :], NB),
                                            over_t(tile_place[:, 1, q * NB:(q + 1) * NB], P), ALU.is_equal
                                            ).then_inc(s.place_hot, 1)
                dve.wait_ge(s.inverse, 1)
                inv = psum[:, 2, 0:3 * (NS + 1)].rearrange("p (a s) -> p a s", a=3)
                with nc.allow_low_precision("whole numbers below 4096"):
                    nc.vector.reduce_sum(source[:, :], inv[:, 1:3, :].rearrange("p a s -> p s a"), AX_X
                                         ).then_inc(s.sources, 1)
                link(nc.vector.tensor_tensor(passed[:, :, :], over_t(slots[:, :], E), over_first(tiles_upto[:, 1:1 + E], NS + 1), ALU.is_ge))
                link(nc.vector.reduce_sum(owner_f[:, :], passed[:, :, :], AX_X))
                nc.vector.tensor_scalar(owner[:, :], owner_f[:, :], float(E - 1), float(REC), ALU.min, ALU.mult
                                        ).then_inc(s.table, 1)
                link(nc.vector.tensor_tensor(taken_row[:, :], inv[:, 0, :], spare_row[:, :], ALU.mult))
                link(nc.vector.tensor_tensor(empty_row[:, :], spare_row[:, :], taken_row[:, :], ALU.subtract))
                dve.wait_ge(s.sources, 1)
                nc.vector.tensor_tensor(target[:, :], source[:, :], empty_row[:, :], ALU.add).then_inc(s.targets, 1)

                if n == 0:
                    dve.wait_ge(attn_loaded, 80)
                    nc.vector.tensor_tensor(proj_wide[:, :, :], over_first(proj_sb[:, :], H),
                                            over_t(head_block[:, :], M), ALU.mult).then_inc(wide_ready, 1)
                def scaled(i, o, par):
                    dve.wait_ge(s.rows_turned, i + (o + 1))
                    dve.wait_ge(s.weights, i + (o + 1))
                    nc.vector.tensor_scalar(lnT[:, par, :], psum[:, par, 0:P], rec[:, ring(o), GG:GG + 1],
                                            rec[:, ring(o), BB:BB + 1], ALU.mult, ALU.add).then_inc(s.inputs, 1)

                def keep(i, o):
                    nc.vector.scalar_tensor_tensor(out=base[:, ring(o), :], in0=rec[:, ring(o), B2:B2 + D],
                                                   scalar=rows_in[:, ring(o), HALF_ALPHA:ROW],
                                                   in1=rows_in[:, ring(o), KEPT:KEPT + D],
                                                   op0=ALU.mult, op1=ALU.add).then_inc(s.inputs, 1)
                    nc.vector.tensor_copy(half_alpha[:, ring(o):ring(o) + 1], rows_in[:, ring(o), HALF_ALPHA:ROW]
                                          ).then_inc(s.inputs, 1)

                def relu(i, o, par):
                    dve.wait_ge(s.up, 2 * (i + o) + 2)
                    for c in range(FC // 2, FC):
                        nc.vector.tensor_scalar(hid[:, par, c, :], psum[:, 5 + 2 * par, (c - 2) * P:(c - 1) * P],
                                                rec[:, ring(o), B1 + c:B1 + c + 1], 0.0, ALU.add, ALU.max
                                                ).then_inc(s.relu_dve, 1)

                def result(i, o, par):
                    dve.wait_ge(s.down, i + (o + 1))
                    if not early(i, o, 4):
                        dve.wait_ge(s.rows_stored[ring(o)], ring_value(i, o - 4))
                    nc.vector.scalar_tensor_tensor(out=rows_out[:, ring(o), :], in0=psum[:, 2 + par, 0:D],
                                                   scalar=half_alpha[:, ring(o):ring(o) + 1],
                                                   in1=base[:, ring(o), :], op0=ALU.mult, op1=ALU.add
                                                   ).then_inc(s.rows_out, 1)

                def tile_step(i, o):
                    if not (isinstance(i, int) and i + o == NS - 1):
                        scaled(i, o + 1, o % 2)
                    relu(i, o, (1 + o) % 2)
                    if not (isinstance(i, int) and i + o == NS - 1):
                        keep(i, o + 1)
                    if not early(i, o, 1):
                        result(i, o - 1, o % 2)

                scaled(1, -1, 0)
                keep(1, -1)
                for o in range(-1, 4):
                    tile_step(1, o)
                with dve.Fori(LOOP_FROM, LOOP_TO - 3, 4) as i:
                    for o in range(4):
                        tile_step(i, o)
                for o in range(2):
                    tile_step(LOOP_TO, o)
                dve.wait_ge(s.inputs, 3 * NS)
                result(LOOP_TO, 1, 0)

                def split_x(fours_before):
                    dve.wait_ge(x_high_ready, fours_before + 1)
                    nc.vector.tensor_tensor(xaT_low[:, :, :].rearrange("p k t -> p (k t)"), psum[:, 0, :],
                                            xaT_high[:, :, :].rearrange("p k t -> p (k t)").bitcast(F32),
                                            ALU.subtract).then_inc(x_low_ready, 1)

                if n == 1:
                    continue

                for j in range(4):
                    dve.wait_ge(w_high_ready, j + 1)
                    at = slice((j % 2) * 512, (j % 2 + 1) * 512)
                    nc.vector.tensor_tensor(w_low[:, j // 2, at], psum[:, 4 + j, :],
                                            w_high[:, j // 2, at].bitcast(F32), ALU.subtract
                                            ).then_inc(w_low_ready, 1)
                dve.wait_ge(new_x_loaded[0], 16)
                norm_stats(tiles_of(x, 0), stats_a, mv_a, a_stats, a_aggr, 0)
                norm_apply(tiles_of(x, 0), tiles_of(xa, 0), mv_a, dev_a[:, :], rstd_a[:, :],
                           a_dev, a_rstd, a_norm, 0)
                split_x(0)
                for q in range(1, NT // NB):
                    dve.wait_ge(new_x_loaded[q], 16)
                dve.wait_ge(filled, 13)
                dve.wait_ge(consts, 11)

                def mask(b, c, quad):
                    dve.wait_ge(scored, b * (4 * CHUNKS) + (4 * c + quad + 1))
                    nc.vector.tensor_tensor(scores[:, c % 2, quad, :, :],
                                            psum[:, 2 + quad, :].rearrange("p (r t) -> p r t", t=P),
                                            over_first(causal[:, :], NB), ALU.mult).then_inc(masked, 1)

                ctx4 = psum[:, 6, 0:2 * P].rearrange("p (r w) -> p r w", w=32)[:, :, 0:18].rearrange(
                    "p r (a w) -> p r a w", a=2)

                def divide(b, c):
                    dve.wait_ge(o_turned, b * CHUNKS + (c + 1))
                    nc.vector.tensor_scalar(den[:, :, :].unsqueeze(3), ctx4[:, :, :, HD:HD + 1], DEN_EPS, None,
                                            ALU.add).then_inc(den_ready, 1)
                    dve.wait_ge(den_ready, b * CHUNKS + (c + 1))
                    nc.vector.reciprocal(inv_den[:, :, :], den[:, :, :]).then_inc(inv_ready, 1)
                    dve.wait_ge(inv_ready, b * CHUNKS + (c + 1))
                    nc.vector.tensor_tensor(heads_out[:, :, :, :], ctx4[:, :, :, 0:HD],
                                            inv_den[:, :, :].unsqueeze(3).broadcast_to([P, PAIRS, 2, HD]),
                                            ALU.mult).then_inc(heads_ready, 1)

                def add_state(b, c):
                    dve.wait_ge(stateT_done, b * (CHUNKS - 1) + (c + 1))
                    sums = psum[:, 7, 0:2 * P].rearrange("p (h m) -> p h m", m=P)
                    if c == 0:
                        nc.vector.tensor_copy(stateT[:, :, :], sums).then_inc(stateT_added, 1)
                    else:
                        dve.wait_ge(stateT_added, b * (CHUNKS - 1) + c)
                        nc.vector.tensor_tensor(stateT[:, :, :], sums, stateT[:, :, :], ALU.add
                                                ).then_inc(stateT_added, 1)

                def split_state(b, c):
                    dve.wait_ge(state_turned, b * (CHUNKS - 1) + (c + 1))
                    dve.wait_ge(state_ready, b * CHUNKS + (c + 1))
                    turned = psum[:, 7, 0:2 * P].rearrange("p (r w) -> p r w", w=32)
                    nc.vector.tensor_copy(state[0:64, :, 0:9], turned[0:64, :, 0:9])
                    nc.vector.tensor_copy(state[64:P, :, 9:18], turned[64:P, :, 9:18]).then_inc(state_ready, 1)

                def add_out(b, c):
                    dve.wait_ge(projected, b * CHUNKS + (c + 1))
                    if c > 0:
                        dve.wait_ge(residual, b * CHUNKS + c)
                    nc.vector.tensor_tensor(proj_out[:, :], psum[:, 6, 0:D], out_bias[:, :], ALU.add
                                            ).then_inc(projected_sb, 1)
                    dve.wait_ge(projected_sb, b * CHUNKS + (c + 1))
                    at = bass.ds(b * CHUNKS + c, 1)
                    nc.vector.tensor_tensor(x[:, at, :], x[:, at, :], proj_out[:, :].unsqueeze(1), ALU.add
                                            ).then_inc(residual, 1)

                with dve.Fori(0, B) as b:
                    nc.vector.memset(state[:, :, :], 0.0).then_inc(state_ready, 1)
                    for g in range(GROUPS):
                        done = NB * g - 1
                        if g > 0:
                            divide(b, done)
                            add_state(b, done)
                            split_state(b, done)
                            add_out(b, done)
                            dve.wait_ge(residual, b * CHUNKS + NB * g)
                        second_stats(b * GROUPS + g)
                        second_apply(b * GROUPS + g)
                        for quad in range(4):
                            mask(b, NB * g, quad)
                        blocks = b * GROUPS + (g + 1)
                        for k in range(NB):
                            c = NB * g + k
                            next_x = tiles_of(x_all, (blocks + 1) * NB)
                            if k == 0:
                                norm_stats(next_x, stats_a, mv_a, a_stats, a_aggr, blocks)
                            if k == 1:
                                norm_apply(next_x, tiles_of(xa, 0), mv_a, dev_a[:, :], rstd_a[:, :],
                                           a_dev, a_rstd, a_norm, blocks)
                            if k < NB - 1:
                                mask(b, c + 1, 0)
                                mask(b, c + 1, 1)
                                divide(b, c)
                                add_state(b, c)
                                mask(b, c + 1, 2)
                                split_state(b, c)
                                add_out(b, c)
                                mask(b, c + 1, 3)
                            else:
                                split_x(blocks)
                                if g == GROUPS - 1:
                                    divide(b, c)
                                    add_out(b, c)
                    dve.wait_ge(residual, b * CHUNKS + CHUNKS)


_ORDER = ["L0_attn_x", "L0_attn_qkv_w", "L0_attn_qkv_b", "L0_attn_out_w", "L0_attn_out_b", "L0_attn_proj",
          "L0_ffn_centroids", "L0_ffn_ln_g", "L0_ffn_ln_b", "L0_ffn_w1", "L0_ffn_b1", "L0_ffn_w2", "L0_ffn_b2"]


def kernel(**inputs):
    import numpy as _np
    import concourse.bacc as _bacc
    from concourse import mybir as _mybir
    from concourse.bass_utils import run_bass_kernel_spmd as _run

    nc = _bacc.Bacc("TRN2", target_bir_lowering=False, num_devices=1)
    arrays, args = {}, []
    for name in _ORDER:
        a = _np.ascontiguousarray(inputs[name])
        arrays[f"in_{name}"] = a
        args.append(nc.dram_tensor(f"in_{name}", a.shape, _mybir.dt.from_np(a.dtype), kind="ExternalInput").ap())
    shape = tuple(inputs["L0_attn_x"].shape)
    out = nc.dram_tensor("out_x", result_rows(shape, inputs["L0_ffn_centroids"].shape[0]), F32,
                         kind="ExternalOutput").ap()
    macaron_block(nc, *args, out)
    r = _run(nc, [arrays], core_ids=[0])
    tokens = shape[0] * shape[1]
    return r.results[0]["out_x"][:tokens].reshape(shape)
```
